# Optimizing a Trainium2 kernel written in Bass

```python
import numpy as np
import jax
import jax.numpy as jnp

def _softmax(x, axis=-1):
    return jax.nn.softmax(x, axis=axis)

def _gelu(x):
    return jax.nn.gelu(x, approximate=True)

def _silu(x):
    return jax.nn.silu(x)

def _sigmoid(x):
    return jax.nn.sigmoid(x)

def _layernorm(x, axis=-1, eps=1e-05):
    m = jnp.mean(x, axis=axis, keepdims=True)
    v = jnp.var(x, axis=axis, keepdims=True)
    return (x - m) / jnp.sqrt(v + eps)

def _scatter_add(tgt, idx, src, axis=0):
    return tgt.at[idx].add(src)

def _segment_sum(src, seg, n):
    return jax.ops.segment_sum(src, seg, n)
kernel_name = 'mk_dlrm_tower_d1_rec_r8_31a26a'

def setup_inputs(seed: int=0):
    np.random.seed(seed)
    _w = jnp.asarray

    def _rec_inputs():
        import jax
        import jax.numpy as jnp
        _tk = jax.random.key(seed)
        ids = jnp.stack([jax.random.randint(jax.random.fold_in(_tk, 200 + f), (2048,), 0, v, jnp.int32) for f, v in enumerate([12500, 12500, 1000, 1250, 12500, 12500, 1000, 1000, 1250, 12500, 1000, 125000, 12500, 12500, 1250, 12500, 1000, 12500, 1250, 1000, 1000, 1000, 1000, 1000, 1000, 1000])], axis=1)
        tbl_0 = 0.05 * jax.random.normal(jax.random.fold_in(_tk, 500 + 0), (12500, 128), jnp.float32)
        tbl_1 = 0.05 * jax.random.normal(jax.random.fold_in(_tk, 500 + 1), (12500, 128), jnp.float32)
        tbl_2 = 0.05 * jax.random.normal(jax.random.fold_in(_tk, 500 + 2), (1000, 128), jnp.float32)
        tbl_3 = 0.05 * jax.random.normal(jax.random.fold_in(_tk, 500 + 3), (1250, 128), jnp.float32)
        tbl_4 = 0.05 * jax.random.normal(jax.random.fold_in(_tk, 500 + 4), (12500, 128), jnp.float32)
        tbl_5 = 0.05 * jax.random.normal(jax.random.fold_in(_tk, 500 + 5), (12500, 128), jnp.float32)
        tbl_6 = 0.05 * jax.random.normal(jax.random.fold_in(_tk, 500 + 6), (1000, 128), jnp.float32)
        tbl_7 = 0.05 * jax.random.normal(jax.random.fold_in(_tk, 500 + 7), (1000, 128), jnp.float32)
        tbl_8 = 0.05 * jax.random.normal(jax.random.fold_in(_tk, 500 + 8), (1250, 128), jnp.float32)
        tbl_9 = 0.05 * jax.random.normal(jax.random.fold_in(_tk, 500 + 9), (12500, 128), jnp.float32)
        tbl_10 = 0.05 * jax.random.normal(jax.random.fold_in(_tk, 500 + 10), (1000, 128), jnp.float32)
        tbl_11 = 0.05 * jax.random.normal(jax.random.fold_in(_tk, 500 + 11), (125000, 128), jnp.float32)
        tbl_12 = 0.05 * jax.random.normal(jax.random.fold_in(_tk, 500 + 12), (12500, 128), jnp.float32)
        tbl_13 = 0.05 * jax.random.normal(jax.random.fold_in(_tk, 500 + 13), (12500, 128), jnp.float32)
        tbl_14 = 0.05 * jax.random.normal(jax.random.fold_in(_tk, 500 + 14), (1250, 128), jnp.float32)
        tbl_15 = 0.05 * jax.random.normal(jax.random.fold_in(_tk, 500 + 15), (12500, 128), jnp.float32)
        tbl_16 = 0.05 * jax.random.normal(jax.random.fold_in(_tk, 500 + 16), (1000, 128), jnp.float32)
        tbl_17 = 0.05 * jax.random.normal(jax.random.fold_in(_tk, 500 + 17), (12500, 128), jnp.float32)
        tbl_18 = 0.05 * jax.random.normal(jax.random.fold_in(_tk, 500 + 18), (1250, 128), jnp.float32)
        tbl_19 = 0.05 * jax.random.normal(jax.random.fold_in(_tk, 500 + 19), (1000, 128), jnp.float32)
        tbl_20 = 0.05 * jax.random.normal(jax.random.fold_in(_tk, 500 + 20), (1000, 128), jnp.float32)
        tbl_21 = 0.05 * jax.random.normal(jax.random.fold_in(_tk, 500 + 21), (1000, 128), jnp.float32)
        tbl_22 = 0.05 * jax.random.normal(jax.random.fold_in(_tk, 500 + 22), (1000, 128), jnp.float32)
        tbl_23 = 0.05 * jax.random.normal(jax.random.fold_in(_tk, 500 + 23), (1000, 128), jnp.float32)
        tbl_24 = 0.05 * jax.random.normal(jax.random.fold_in(_tk, 500 + 24), (1000, 128), jnp.float32)
        tbl_25 = 0.05 * jax.random.normal(jax.random.fold_in(_tk, 500 + 25), (1000, 128), jnp.float32)
        _rk = jax.random.fold_in(_tk, 7)
        r_dense = -0.000520686 + 1.00062 * jax.random.normal(jax.random.fold_in(_rk, 101), (2048, 128), jnp.float32)
        W_top1 = 0.0456912 * jax.random.normal(jax.random.fold_in(_tk, 801), (479, 512), jnp.float32)
        W_top2 = 0.0441942 * jax.random.normal(jax.random.fold_in(_tk, 802), (512, 256), jnp.float32)
        W_top3 = 0.0625 * jax.random.normal(jax.random.fold_in(_tk, 803), (256, 1), jnp.float32)
        b_top1 = jnp.zeros((512,), jnp.float32)
        b_top2 = jnp.zeros((256,), jnp.float32)
        return (r_dense, ids, tbl_0, tbl_1, tbl_2, tbl_3, tbl_4, tbl_5, tbl_6, tbl_7, tbl_8, tbl_9, tbl_10, tbl_11, tbl_12, tbl_13, tbl_14, tbl_15, tbl_16, tbl_17, tbl_18, tbl_19, tbl_20, tbl_21, tbl_22, tbl_23, tbl_24, tbl_25, W_top1, b_top1, W_top2, b_top2, W_top3)
    r_dense, ids, tbl_0, tbl_1, tbl_2, tbl_3, tbl_4, tbl_5, tbl_6, tbl_7, tbl_8, tbl_9, tbl_10, tbl_11, tbl_12, tbl_13, tbl_14, tbl_15, tbl_16, tbl_17, tbl_18, tbl_19, tbl_20, tbl_21, tbl_22, tbl_23, tbl_24, tbl_25, W_top1, b_top1, W_top2, b_top2, W_top3 = _rec_inputs()

    def _L0_rec_setup():
        import jax, jax.numpy as jnp
        import numpy as np
        B, NUM_EMBS, D = (2048, 26, 128)
        key = jax.random.key(seed)
        k1, k2 = jax.random.split(key)
        dense = jax.random.normal(k1, (B, D), dtype=jnp.float32)
        embs = jax.random.normal(k2, (B, NUM_EMBS, D), dtype=jnp.float32)
        return {'dense': dense, 'embs': embs}
    _L0_rec_all = _L0_rec_setup()
    _L0_rec_in = {k: v for k, v in _L0_rec_all.items() if k in ()}
    del _L0_rec_all
    return {'r_dense': r_dense, 'ids': ids, 'tbl_0': tbl_0, 'tbl_1': tbl_1, 'tbl_2': tbl_2, 'tbl_3': tbl_3, 'tbl_4': tbl_4, 'tbl_5': tbl_5, 'tbl_6': tbl_6, 'tbl_7': tbl_7, 'tbl_8': tbl_8, 'tbl_9': tbl_9, 'tbl_10': tbl_10, 'tbl_11': tbl_11, 'tbl_12': tbl_12, 'tbl_13': tbl_13, 'tbl_14': tbl_14, 'tbl_15': tbl_15, 'tbl_16': tbl_16, 'tbl_17': tbl_17, 'tbl_18': tbl_18, 'tbl_19': tbl_19, 'tbl_20': tbl_20, 'tbl_21': tbl_21, 'tbl_22': tbl_22, 'tbl_23': tbl_23, 'tbl_24': tbl_24, 'tbl_25': tbl_25, 'W_top1': W_top1, 'b_top1': b_top1, 'W_top2': W_top2, 'b_top2': b_top2, 'W_top3': W_top3}

def reference(r_dense, ids, tbl_0, tbl_1, tbl_2, tbl_3, tbl_4, tbl_5, tbl_6, tbl_7, tbl_8, tbl_9, tbl_10, tbl_11, tbl_12, tbl_13, tbl_14, tbl_15, tbl_16, tbl_17, tbl_18, tbl_19, tbl_20, tbl_21, tbl_22, tbl_23, tbl_24, tbl_25, W_top1, b_top1, W_top2, b_top2, W_top3):
    import jax
    import jax.numpy as jnp

    def _L0_rec_ref(dense, embs):
        import jax, jax.numpy as jnp
        import numpy as np
        B, NUM_EMBS, D = (2048, 26, 128)
        T = jnp.concatenate([dense[:, None, :], embs], axis=1)
        N = T.shape[1]
        Z = jnp.einsum('bnd,bmd->bnm', T, T)
        iu0, iu1 = jnp.triu_indices(N, k=1)
        return Z[:, iu0, iu1]
    e = jnp.stack([tbl_0[ids[:, 0]], tbl_1[ids[:, 1]], tbl_2[ids[:, 2]], tbl_3[ids[:, 3]], tbl_4[ids[:, 4]], tbl_5[ids[:, 5]], tbl_6[ids[:, 6]], tbl_7[ids[:, 7]], tbl_8[ids[:, 8]], tbl_9[ids[:, 9]], tbl_10[ids[:, 10]], tbl_11[ids[:, 11]], tbl_12[ids[:, 12]], tbl_13[ids[:, 13]], tbl_14[ids[:, 14]], tbl_15[ids[:, 15]], tbl_16[ids[:, 16]], tbl_17[ids[:, 17]], tbl_18[ids[:, 18]], tbl_19[ids[:, 19]], tbl_20[ids[:, 20]], tbl_21[ids[:, 21]], tbl_22[ids[:, 22]], tbl_23[ids[:, 23]], tbl_24[ids[:, 24]], tbl_25[ids[:, 25]]], axis=1)
    z = _L0_rec_ref(r_dense, e)
    z = z.reshape(z.shape[0], -1)
    h = jnp.concatenate([z, r_dense], axis=1)
    h = jnp.maximum(h @ W_top1 + b_top1, 0.0)
    h = jnp.maximum(h @ W_top2 + b_top2, 0.0)
    y = h @ W_top3
    return y

_drawn_inputs = setup_inputs


def setup_inputs(seed=0):
    import zlib

    import numpy as np

    out = dict(_drawn_inputs(seed))
    spreads = {'b_top1': (0.0, 0.1), 'b_top2': (0.0, 0.1)}
    factors = {}
    for name, (base, spread) in spreads.items():
        noise = np.random.default_rng([zlib.crc32(name.encode()), seed]).standard_normal(out[name].shape)
        drawn = base * np.exp(spread * noise) if base else spread * noise
        out[name] = jnp.asarray(drawn.astype(out[name].dtype))
    for name, factor in factors.items():
        out[name] = (out[name] * factor).astype(out[name].dtype)
    return out
```

```python
from contextlib import ExitStack

import concourse.bass as bass
from concourse import mybir

F32 = mybir.dt.float32
F32R = mybir.dt.float32r
F16 = mybir.dt.float16
I32 = mybir.dt.int32
U32 = mybir.dt.uint32
ALU = mybir.AluOpType
ACT = mybir.ActivationFunctionType

P = 128
ONEHOT = 8
RAWS = 4
MAX_ROUND = 4
LOW_BITS = 12


def plan(table_rows):
    nt = len(table_rows)
    least = min(table_rows)
    small = [f for f in range(nt) if table_rows[f] == least]
    onehot = sorted(small[-(ONEHOT - 1):] + small[:1])
    runs = []
    for n in range(nt + 1):
        if n - 1 in onehot:
            continue
        if runs and runs[-1][-1] == n - 1 and len(runs[-1]) < MAX_ROUND:
            runs[-1].append(n)
        else:
            runs.append([n])
    return onehot, runs


def pair_weight_pieces(nv, half, per_chunk):
    def triu(n, m):
        return n * nv - n * (n + 1) // 2 + m - n - 1

    pieces = []
    for m in range(nv - 1):
        pieces.append((triu(m, m + 1), min(half, nv - 1 - m), m // per_chunk, m % per_chunk * half, 1))
    for n in range(half):
        m = nv - half + n
        while m < nv:
            cnt = min(nv - m, per_chunk - m % per_chunk)
            pieces.append((triu(n, m), cnt, m // per_chunk, m % per_chunk * half + n + nv - m - 1, half - 1))
            m += cnt
    return pieces


def dlrm_tower(nc, r_dense, ids, tables, W1, b1, W2, b2, W3, out):
    B, NT = ids.shape
    D = r_dense.shape[1]
    F1, F2 = W1.shape[1], W2.shape[1]
    NV = NT + 1
    HALF = (NV - 1) // 2
    PAIRS = NV * HALF
    TILES = B // P
    UNITS = TILES // 2
    Q = 2 * P
    NJ, NI = 4, P // 4
    HI = NI // 2
    F1C, F2C = F1 // P, F2 // P
    PC = -(-PAIRS // P)
    MC = NV // PC
    KP = MC * HALF
    WIDE = NV + HALF
    onehot, rounds = plan([t.shape[0] for t in tables])
    NR = len(rounds)
    flat = [n for r in rounds for n in r]
    place = {n: i for i, n in enumerate(flat)}
    V = tables[onehot[0]].shape[0]
    CH = 8
    VP = V // CH
    assert VP * CH == V and VP <= P and V <= 2048 and D == P and UNITS % 2 == 0 and NR % 2 == 1
    assert NV % 2 == 1 and MC * PC == NV and KP <= P and HI * NV <= 512
    w1_pieces = pair_weight_pieces(NV, HALF, MC)
    SHUFFLED = 16 * NJ * PC
    WEIGHTS = 16 * (len(w1_pieces) + 5)
    dots = nc.dram_tensor("dots", (2, NJ, NI * WIDE * Q // NJ), F32, kind="Internal").ap()

    with ExitStack() as ctx:
        def sb(name, shape, dt):
            return ctx.enter_context(nc.sbuf_tensor(name, shape, dt))

        def psum(name, shape, dt):
            return ctx.enter_context(nc.psum_tensor(name, shape, dt))

        def sem(name):
            return ctx.enter_context(nc.semaphore(name))

        T = sb("T", [P, 2, Q, NV], F32)
        tab_hi = sb("tab_hi", [P, ONEHOT, CH, D], F32R)
        tab_lo = sb("tab_lo", [P, ONEHOT, CH, D], F32R)
        hot = sb("hot", [P, 2, CH, Q], F32R)
        rows = sb("rows", [P, 2, len(flat), D], F32)
        gram = sb("gram", [P, NV, Q // NJ], F32)
        pairs = sb("pairs", [P, PC, Q], F32)
        w1 = sb("w1", [P, PC + 1, F1], F32)
        w2 = sb("w2", [P, F1C, F2], F32)
        w3 = sb("w3", [P, F2C], F32)
        bias1 = sb("bias1", [P, F1C], F32)
        bias2 = sb("bias2", [P, F2C], F32)
        h1 = sb("h1", [P, F1C, Q], F32)
        h2 = sb("h2", [P, F2C, 2, P], F32)
        y = sb("y", [P, TILES], F32)
        ids_all = sb("ids_all", [P, TILES, NT], I32)
        ids_hot = sb("ids_hot", [P, ONEHOT * (TILES - 1) + P], F32)
        ids_t = sb("ids_t", [P, UNITS + 1, Q], F16)
        idx = sb("idx", [P, 4, NT], I32)
        ident = sb("ident", [P, P], F32)
        row_no = sb("row_no", [P, CH], F32)
        pick = sb("pick", [P, ONEHOT, P], F16)
        stage = T[:, 1].rearrange("p q n -> p (q n)")
        raw = [stage[:VP, i * CH * D:(i + 1) * CH * D] for i in range(RAWS)]
        top = [stage[:VP, (RAWS + i) * CH * D:(RAWS + i + 1) * CH * D] for i in range(2)]
        look_ps = psum("look_ps", [P, 2, 512], F32)
        ids_ps = psum("ids_ps", [P, 2, 512], F32)
        gram_ps = psum("gram_ps", [P, 2, 512], F32)
        mlp_ps = psum("mlp_ps", [P, 2, 2, Q], F32)

        idx_landed = [sem(f"idx_landed{i}") for i in range(4)]
        dense_landed = [sem(f"dense_landed{i}") for i in range(2)]
        rows_landed = [[sem(f"rows_landed{i}_{r}") for r in range(NR)] for i in range(2)]
        ids_landed = sem("ids_landed")
        raw_landed = [sem(f"raw_landed{i}") for i in range(RAWS)]
        weights_landed = sem("weights_landed")
        dots_stored = sem("dots_stored")
        shuffled = sem("shuffled")
        stored = sem("stored")
        tiles_begun = sem("tiles_begun")
        ident_zero = sem("ident_zero")
        ident_ready = sem("ident_ready")
        pick_zero = sem("pick_zero")
        pick_ready = sem("pick_ready")
        row_no_ready = sem("row_no_ready")
        ids_hot_ready = sem("ids_hot_ready")
        ids_t_zero = sem("ids_t_zero")
        ids_turned = sem("ids_turned")
        ids_t_ready = sem("ids_t_ready")
        top_ready = sem("top_ready")
        hi_ready = sem("hi_ready")
        lo_ready = sem("lo_ready")
        ids_spread = sem("ids_spread")
        hot_ready = sem("hot_ready")
        hot_looked = sem("hot_looked")
        turned = sem("turned")
        look_free = sem("look_free")
        gram_done = sem("gram_done")
        gram_free = sem("gram_free")
        l1_done = sem("l1_done")
        h1_ready = sem("h1_ready")
        l2_done = sem("l2_done")
        h2_ready = sem("h2_ready")
        l3_done = sem("l3_done")
        y_ready = sem("y_ready")

        ids_v = ids.rearrange("(p t) f -> p t f", p=P)
        dense_v = r_dense.rearrange("(p t) d -> p t d", p=P)
        T_tile = [[T[:, par].rearrange("p (j l i) n -> p l n j i", j=NJ, l=2)[:, l] for l in range(2)]
                  for par in range(2)]
        QJ = Q // NJ

        def tile_of(it, a, l):
            return 4 * it + 2 * a + l

        def ids_bank(u):
            banks = [mlp_ps[:, 0].rearrange("p f q -> p (f q)"), mlp_ps[:, 1].rearrange("p f q -> p (f q)"),
                     look_ps[:, 0], look_ps[:, 1]]
            return banks[u // 2][:, u % 2 * Q:(u % 2 + 1) * Q]

        PER_TILE = NR + ONEHOT // 2

        def use_of(it, a, l, i, last=False):
            return ONEHOT + 2 * PER_TILE * (2 * it + a) + (NR if last else PER_TILE) * l + i

        def bank_of(l, i):
            return (PER_TILE * l + i) % 2

        assert ONEHOT % 2 == 0 and (PER_TILE - NR) % 2 == 0

        block = ctx.enter_context(nc.Block())

        @block.sync
        def _(sp):
            def load_idx(it, a, l):
                t, s = tile_of(it, a, l), (2 * a + l) % 4
                sp.dma_start(idx[:, s, :], ids_v[:, bass.ds(t, 1), :].rearrange("p a f -> p (a f)")
                             ).then_inc(idx_landed[s], 16)

            def load_dense(it, a, l):
                t = tile_of(it, a, l)
                sp.dma_start(rows[:, l, place[0], :], dense_v[:, bass.ds(t, 1), :].rearrange("p a d -> p (a d)")
                             ).then_inc(dense_landed[l], 16)

            def load_raw(k):
                if k >= RAWS:
                    sp.wait_ge(lo_ready, k - RAWS + 1)
                sp.dma_start(raw[k % RAWS], tables[onehot[k]].rearrange("(p c) d -> p (c d)", c=CH)
                             ).then_inc(raw_landed[k % RAWS], 16)

            def load_weights():
                for w_row, cnt, c, r, step in w1_pieces:
                    sp.dma_start(w1[r:r + step * (cnt - 1) + 1:step, c, :], W1[w_row:w_row + cnt, :]
                                 ).then_inc(weights_landed, 16)
                sp.dma_start(w1[:, PC, :], W1[PAIRS:PAIRS + D, :]).then_inc(weights_landed, 16)
                sp.dma_start(w2[:], W2.rearrange("(c p) f -> p c f", p=P)).then_inc(weights_landed, 16)
                with nc.allow_non_contiguous_dma(reason="a few hundred words"):
                    sp.dma_start(w3[:], W3.rearrange("(c p) o -> p (c o)", p=P)).then_inc(weights_landed, 16)
                    sp.dma_start(bias1[:], b1.rearrange("(c p) -> p c", p=P)).then_inc(weights_landed, 16)
                    sp.dma_start(bias2[:], b2.rearrange("(c p) -> p c", p=P)).then_inc(weights_landed, 16)

            def unit(it, a, last=False):
                if not last:
                    load_idx(it, a + 1, 0)
                for l in range(2):
                    if not last:
                        sp.wait_ge(turned, 2 * NR + NR * (tile_of(it, a, l) + 1))
                        load_dense(it, a + 1, l)
                        if l == 0:
                            load_idx(it, a + 1, 1)
                sp.wait_ge(gram_free, 2 + 4 * (2 * it + a + 1))
                rows_v = dots[a % 2].rearrange("j (m n i) -> (j m) n i", m=NI, n=WIDE)
                sp.dma_start(rows_v[:, 0:NV, :], gram[:]).then_inc(dots_stored, 16)
                sp.dma_start(rows_v[:, NV:WIDE, :], gram[:, 0:HALF]).then_inc(dots_stored, 16)
                sp.wait_ge(dots_stored, 32 * (2 * it + a + 1))
                for c in range(PC):
                    first, step = MC * c * WIDE + MC * c + 1, WIDE + 1
                    for j in range(NJ):
                        src = dots[a % 2, j, first * QJ:(first + MC * step) * QJ].rearrange("(m x) -> m x", m=MC)
                        sp.dma_start(pairs[0:KP, c, j * QJ:(j + 1) * QJ],
                                     src[:, 0:HALF * QJ].rearrange("m (k i) -> m k i", i=QJ)).then_inc(shuffled, 16)

            load_idx(0, 0, 0)
            sp.dma_start(ids_all[:], ids_v).then_inc(ids_landed, 16)
            load_raw(0)
            load_raw(1)
            load_idx(0, 0, 1)
            load_dense(0, 0, 0)
            load_dense(0, 0, 1)
            for k in range(2, ONEHOT):
                load_raw(k)
            load_weights()
            unit(0, 0)
            with sp.Fori(0, UNITS // 2 - 1) as it:
                unit(it, 1)
                unit(it, 2)
            unit(UNITS // 2 - 1, 1, last=True)
            sp.wait_ge(y_ready, UNITS)
            sp.dma_start(out.rearrange("(p t) o -> p (t o)", p=P), y[:]).then_inc(stored, 16)
            sp.wait_ge(stored, 16)

        @block.gpsimd
        def _(pool):
            nc.gpsimd.memset(ident[:], 0.0).then_inc(ident_zero, 1)
            pool.wait_ge(ident_zero, 1)
            nc.gpsimd.affine_select(out=ident[:], in_=ident[:], compare_op=ALU.not_equal, fill=1.0, base=0,
                                    pattern=[[-1, P]], channel_multiplier=1).then_inc(ident_ready, 1)
            nc.gpsimd.iota(row_no[:], pattern=[[1, CH]], base=0, channel_multiplier=CH,
                           allow_small_or_imprecise_dtypes=True).then_inc(row_no_ready, 1)
            pool.wait_ge(pick_zero, 1)
            nc.gpsimd.affine_select(out=pick[:], in_=pick[:], compare_op=ALU.not_equal, fill=1.0, base=0,
                                    pattern=[[-1, ONEHOT], [0, P]], channel_multiplier=1).then_inc(pick_ready, 1)

            def gather(it, a, l):
                t, s = tile_of(it, a, l), (2 * a + l) % 4
                pool.wait_ge(idx_landed[s], 16 * (it + (2 * a + l) // 4 + 1))
                pool.wait_ge(turned, NR * (t + 1))
                pool.sem_inc(tiles_begun, 1)
                for r in range(NR):
                    for n in rounds[r]:
                        if n == 0:
                            continue
                        pool.indirect_dma_start(
                            rows[:, l, place[n], :], None, tables[n - 1],
                            bass.IndirectOffsetOnAxis(ap=idx[:, s, n - 1:n].bitcast(U32), axis=0),
                        ).then_inc(rows_landed[l][r], 16)

            with pool.Fori(0, UNITS // 2) as it:
                for a in range(2):
                    for l in range(2):
                        gather(it, a, l)

        @block.vector
        def _(dve):
            nc.vector.memset(pick[:], 0.0).then_inc(pick_zero, 1)
            for h in range(2):
                nc.vector.memset(gram_ps[:, h, :], 0.0).then_inc(gram_free, 1)
            nc.vector.memset(ids_t[:], 0.0).then_inc(ids_t_zero, 1)
            nc.vector.memset(ids_hot[:, ONEHOT * TILES:], 0.0).then_inc(ids_hot_ready, 1)
            dve.wait_ge(ids_landed, 16)
            ids_hot_v = ids_hot[:, 0:ONEHOT * TILES].rearrange("p (t k) -> p t k", k=ONEHOT)
            nc.vector.tensor_copy(ids_hot_v[:, :, 0:1], ids_all[:, :, onehot[0]:onehot[0] + 1]).then_inc(ids_hot_ready, 1)
            nc.vector.tensor_copy(ids_hot_v[:, :, 1:], ids_all[:, :, onehot[1]:onehot[-1] + 1]).then_inc(ids_hot_ready, 1)

            def split(k):
                dve.wait_ge(raw_landed[k % RAWS], 16 * (k // RAWS + 1))
                if k >= 2:
                    dve.wait_ge(hi_ready, k - 1)
                nc.vector.tensor_scalar(top[k % 2].bitcast(I32), raw[k % RAWS].bitcast(I32), -(1 << LOW_BITS), None,
                                        ALU.bitwise_and).then_inc(top_ready, 1)
                dve.wait_ge(top_ready, k + 1)
                nc.vector.tensor_tensor(tab_lo[:VP, k].rearrange("p c d -> p (c d)"), raw[k % RAWS], top[k % 2],
                                        ALU.subtract).then_inc(lo_ready, 1)

            def compare(g, k):
                dve.wait_ge(ids_spread, g + 1)
                if not (isinstance(g, int) and g < 2):
                    dve.wait_ge(hot_looked, g - 1)
                nc.vector.tensor_tensor(
                    hot[:VP, k % 2], ids_ps[:VP, k % 2, 0:Q].unsqueeze(1).to_broadcast([VP, CH, Q]),
                    row_no[:VP, :].unsqueeze(2).to_broadcast([VP, CH, Q]), ALU.is_equal).then_inc(hot_ready, 1)

            def gram_out(it, a, l):
                for h in range(2):
                    x = 2 * tile_of(it, a, l) + h
                    dve.wait_ge(gram_done, x + 1)
                    i0 = l * NI + h * HI
                    nc.vector.tensor_copy(
                        gram[:, :, i0:i0 + HI],
                        gram_ps[:, h, 0:HI * NV].rearrange("p (i n) -> p n i", n=NV)).then_inc(gram_free, 1)

            def unit(it, a, last=False):
                g = ONEHOT * (2 * it + a + 1)
                gram_out(it, a, 0)
                if not last:
                    for k in range(2, ONEHOT // 2 + 2):
                        compare(g + k, k)
                gram_out(it, a, 1)
                if not last:
                    for k in range(ONEHOT // 2 + 2, ONEHOT):
                        compare(g + k, k)

            def next_compares(it, a):
                for k in range(2):
                    compare(ONEHOT * (2 * it + a + 1) + k, k)

            dve.wait_ge(row_no_ready, 1)
            split(0)
            compare(0, 0)
            for k in range(1, ONEHOT):
                split(k)
                compare(k, k)
            next_compares(0, 0)
            unit(0, 0)
            with dve.Fori(0, UNITS // 2 - 1) as it:
                next_compares(it, 1)
                unit(it, 1)
                next_compares(it, 2)
                unit(it, 2)
            unit(UNITS // 2 - 1, 1, last=True)

        @block.scalar
        def _(act):
            nc.scalar.nop().then_inc(look_free, 2)
            act.wait_ge(ids_t_zero, 1)
            ids_t_v = ids_t[:].rearrange("p u (j l i) -> p u l j i", j=NJ, l=2)
            for u in range(UNITS):
                act.wait_ge(ids_turned, u // 2 + 1)
                nc.scalar.copy(ids_t_v[0:ONEHOT, u], ids_bank(u)[0:ONEHOT].rearrange("p (l j i) -> p l j i", l=2, j=NJ)
                               ).then_inc(ids_t_ready, 1)

            def hi_out(k):
                act.wait_ge(top_ready, k + 1)
                nc.scalar.copy(tab_hi[:VP, k].rearrange("p c d -> p (c d)"), top[k % 2]).then_inc(hi_ready, 1)

            def hot_out(it, a, k, bank):
                act.wait_ge(hot_looked, ONEHOT * (2 * it + a) + k + 1)
                nc.scalar.copy(T[:, a % 2, :, onehot[k] + 1], look_ps[:, bank, 0:Q]).then_inc(look_free, 1)

            def turn_out(it, a, l):
                for r in range(NR):
                    n, cnt = rounds[r][0], len(rounds[r])
                    act.wait_ge(turned, 2 * NR + NR * tile_of(it, a, l) + r + 1)
                    nc.scalar.copy(T_tile[a % 2][l][:, n:n + cnt],
                                   look_ps[:, bank_of(l, r), 0:cnt * P].rearrange("p (n j i) -> p n j i", n=cnt, j=NJ)
                                   ).then_inc(look_free, 1)

            def h1_out(it, a):
                for f in range(F1C):
                    act.wait_ge(l1_done, F1C // 2 * (2 * it + a) + f // 2 + 1)
                    nc.scalar.activation(h1[:, f], mlp_ps[:, f // 2, f % 2], ACT.Relu, bias=bias1[:, f:f + 1]
                                         ).then_inc(h1_ready, 1)

            def h2_out(it, a):
                act.wait_ge(l2_done, 2 * it + a + 1)
                for f in range(F2C):
                    nc.scalar.activation(h2[:, f].rearrange("p l (j i) -> p j l i", j=NJ),
                                         mlp_ps[:, 0, f].rearrange("p (j l i) -> p j l i", j=NJ, l=2),
                                         ACT.Relu, bias=bias2[:, f:f + 1]
                                         ).then_inc(h2_ready, 1)

            def y_out(it, a):
                act.wait_ge(l3_done, 2 * it + a + 1)
                nc.scalar.copy(y[:, bass.ds(tile_of(it, a, 0), 2)], mlp_ps[:, 1, 0, 0:2]).then_inc(y_ready, 1)

            def unit(it, a, first=False, last=False):
                turn_out(it, a, 0)
                if not first:
                    h1_out(it, a - 1)
                    h2_out(it, a - 1)
                if not last:
                    for k in range(ONEHOT // 2):
                        hot_out(it, a + 1, k, bank_of(0, NR + k))
                if not first:
                    y_out(it, a - 1)
                turn_out(it, a, 1)
                if not last:
                    for k in range(ONEHOT // 2, ONEHOT):
                        hot_out(it, a + 1, k, bank_of(1, NR + k - ONEHOT // 2))

            for k in range(ONEHOT):
                hi_out(k)
                if k >= 1:
                    hot_out(0, 0, k - 1, (k - 1) % 2)
            hot_out(0, 0, ONEHOT - 1, (ONEHOT - 1) % 2)
            act.wait_ge(weights_landed, WEIGHTS)
            unit(0, 0, first=True)
            with act.Fori(0, UNITS // 2 - 1) as it:
                unit(it, 1)
                unit(it, 2)
            end = UNITS // 2 - 1
            unit(end, 1, last=True)
            h1_out(end, 1)
            h2_out(end, 1)
            y_out(end, 1)

        @block.tensor
        def _(pe):
            nc.tensor.nop().then_inc(turned, 2 * NR)

            def spread(it, a, k):
                pe.matmul(ids_ps[:, k % 2, 0:Q], pick[:, k], ids_t[:, unit_no(it, a)], start=True, stop=True
                          ).then_inc(ids_spread, 1)

            def unit_no(it, a):
                return 2 * it + a

            def lookup(it, a, k, use, bank, prologue=False):
                g = ONEHOT * (2 * it + a) + k
                pe.wait_ge(hot_ready, g + 1)
                if k + 2 < ONEHOT:
                    spread(it, a, k + 2)
                else:
                    spread(it, a + 1, k + 2 - ONEHOT)
                if prologue:
                    pe.wait_ge(hi_ready, k + 1)
                    pe.wait_ge(lo_ready, k + 1)
                pe.wait_ge(look_free, use + 1)
                for c in range(CH):
                    for half, w in enumerate((tab_hi, tab_lo)):
                        mm = pe.matmul(look_ps[:, bank, 0:Q], w[:VP, k, c], hot[:VP, k % 2, c],
                                       start=(c == 0 and half == 0), stop=(c == CH - 1 and half == 1))
                mm.then_inc(hot_looked, 1)

            def turn(it, a, l, last=False):
                use = 2 * it + a + 1
                pe.wait_ge(dense_landed[l], 16 * use)
                for r in range(NR):
                    pe.wait_ge(rows_landed[l][r], 16 * (len(rounds[r]) - (0 in rounds[r])) * use)
                    pe.wait_ge(look_free, use_of(it, a, l, r, last) + 1)
                    for i, n in enumerate(rounds[r]):
                        mm = pe.transpose(look_ps[:, bank_of(l, r), i * P:(i + 1) * P], rows[:, l, place[n], :], ident[:])
                    mm.then_inc(turned, 1)

            def products(it, a, l, last=False):
                t = tile_of(it, a, l)
                pe.wait_ge(look_free, 2 + use_of(it, a, l, NR, last))
                for h in range(2):
                    pe.wait_ge(gram_free, 2 * t + h + 1)
                    for i in range(HI):
                        for j in range(NJ):
                            q = (j * 2 + l) * NI + h * HI + i
                            mm = pe.matmul(gram_ps[32 * j:32 * j + NV, h, i * NV:(i + 1) * NV],
                                           T[:, a % 2, q, :], T[:, a % 2, q, 0:NV], start=True, stop=True)
                    mm.then_inc(gram_done, 1)

            def layer1(it, a):
                pe.wait_ge(shuffled, SHUFFLED * (2 * it + a + 1))
                for f in range(F1C):
                    for c in range(PC + 1):
                        kk = P if c == PC else KP
                        rhs = T[:, a % 2, :, 0] if c == PC else pairs[:kk, c]
                        mm = pe.matmul(mlp_ps[:, f // 2, f % 2], w1[:kk, c, f * P:(f + 1) * P], rhs,
                                       start=(c == 0), stop=(c == PC))
                    if f % 2:
                        mm.then_inc(l1_done, 1)

            def layer2(it, a):
                for f in range(F2C):
                    for c in range(F1C):
                        if f == 0:
                            pe.wait_ge(h1_ready, F1C * (2 * it + a) + (c + 1 if c >= 2 else 2))
                        mm = pe.matmul(mlp_ps[:, 0, f], w2[:, c, f * P:(f + 1) * P], h1[:, c],
                                       start=(c == 0), stop=(c == F1C - 1))
                mm.then_inc(l2_done, 1)

            def layer3(it, a):
                pe.wait_ge(h2_ready, F2C * (2 * it + a + 1))
                for l in range(2):
                    for c in range(F2C):
                        mm = pe.matmul(mlp_ps[:, 1, 0, l:l + 1], h2[:, c, l], w3[:, c:c + 1],
                                       start=(c == 0), stop=(c == F2C - 1))
                mm.then_inc(l3_done, 1)

            def unit(it, a, first=False, last=False):
                turn(it, a, 0, last)
                if not first:
                    layer1(it, a - 1)
                products(it, a, 0, last)
                if not first:
                    layer2(it, a - 1)
                if not last:
                    for k in range(ONEHOT // 2):
                        lookup(it, a + 1, k, use_of(it, a, 0, NR + k), bank_of(0, NR + k))
                if not first:
                    layer3(it, a - 1)
                turn(it, a, 1, last)
                products(it, a, 1, last)
                if not last:
                    for k in range(ONEHOT // 2, ONEHOT):
                        i = NR + k - ONEHOT // 2
                        lookup(it, a + 1, k, use_of(it, a, 1, i), bank_of(1, i))

            pe.wait_ge(ident_ready, 1)
            pe.wait_ge(ids_hot_ready, 3)
            for t in range(TILES):
                mm = pe.transpose(ids_bank(t // 2)[:, (t % 2) * P:(t % 2 + 1) * P],
                                  ids_hot[:, t * ONEHOT:t * ONEHOT + P], ident[:])
                if t % 4 == 3:
                    mm.then_inc(ids_turned, 1)
            pe.wait_ge(pick_ready, 1)
            pe.wait_ge(ids_t_ready, UNITS)
            spread(0, 0, 0)
            spread(0, 0, 1)
            for k in range(ONEHOT):
                lookup(0, 0, k, k, k % 2, prologue=True)
            pe.wait_ge(weights_landed, WEIGHTS)
            unit(0, 0, first=True)
            with pe.Fori(0, UNITS // 2 - 1) as it:
                unit(it, 1)
                unit(it, 2)
            end = UNITS // 2 - 1
            unit(end, 1, last=True)
            layer1(end, 1)
            layer2(end, 1)
            layer3(end, 1)


_INS = ['r_dense', 'ids'] + [f'tbl_{i}' for i in range(26)] + ['W_top1', 'b_top1', 'W_top2', 'b_top2', 'W_top3']


def kernel(**inputs):
    import numpy as _np
    import concourse.bacc as _bacc
    from concourse import mybir as _mybir
    from concourse.bass_utils import run_bass_kernel_spmd as _run

    nc = _bacc.Bacc("TRN2", target_bir_lowering=False, num_devices=1)
    arrays, args = {}, []
    for name in _INS:
        a = _np.ascontiguousarray(inputs[name])
        arrays[f"in_{name}_dram"] = a
        args.append(nc.dram_tensor(f"in_{name}_dram", a.shape, _mybir.dt.from_np(a.dtype), kind="ExternalInput").ap())
    out = nc.dram_tensor("out_0_dram", (inputs['r_dense'].shape[0], 1), _mybir.dt.float32, kind="ExternalOutput").ap()
    dlrm_tower(nc, args[0], args[1], args[2:28], *args[28:33], out)
    r = _run(nc, [arrays], core_ids=[0])
    return r.results[0]["out_0_dram"]
```

```python
from contextlib import ExitStack

import concourse.bass as bass
from concourse import mybir

F32 = mybir.dt.float32
F32R = mybir.dt.float32r
F16 = mybir.dt.float16
I32 = mybir.dt.int32
U32 = mybir.dt.uint32
ALU = mybir.AluOpType
ACT = mybir.ActivationFunctionType

P = 128
ONEHOT = 8
RAWS = 4
MAX_ROUND = 4
LOW_BITS = 12


def plan(table_rows):
    nt = len(table_rows)
    least = min(table_rows)
    small = [f for f in range(nt) if table_rows[f] == least]
    onehot = sorted(small[-(ONEHOT - 1):] + small[:1])
    runs = []
    for n in range(nt + 1):
        if n - 1 in onehot:
            continue
        if runs and runs[-1][-1] == n - 1 and len(runs[-1]) < MAX_ROUND:
            runs[-1].append(n)
        else:
            runs.append([n])
    return onehot, runs


def pair_weight_pieces(nv, half, per_chunk):
    def triu(n, m):
        return n * nv - n * (n + 1) // 2 + m - n - 1

    pieces = []
    for m in range(nv - 1):
        pieces.append((triu(m, m + 1), min(half, nv - 1 - m), m // per_chunk, m % per_chunk * half, 1))
    for n in range(half):
        m = nv - half + n
        while m < nv:
            cnt = min(nv - m, per_chunk - m % per_chunk)
            pieces.append((triu(n, m), cnt, m // per_chunk, m % per_chunk * half + n + nv - m - 1, half - 1))
            m += cnt
    return pieces


def dlrm_tower(nc, r_dense, ids, tables, W1, b1, W2, b2, W3, out):
    B, NT = ids.shape
    D = r_dense.shape[1]
    F1, F2 = W1.shape[1], W2.shape[1]
    NV = NT + 1
    HALF = (NV - 1) // 2
    PAIRS = NV * HALF
    TILES = B // P
    UNITS = TILES // 2
    Q = 2 * P
    NJ, NI = 4, P // 4
    HI = NI // 2
    F1C, F2C = F1 // P, F2 // P
    PC = -(-PAIRS // P)
    MC = NV // PC
    KP = MC * HALF
    WIDE = NV + HALF
    onehot, rounds = plan([t.shape[0] for t in tables])
    NR = len(rounds)
    flat = [n for r in rounds for n in r]
    place = {n: i for i, n in enumerate(flat)}
    V = tables[onehot[0]].shape[0]
    CH = 8
    VP = V // CH
    assert VP * CH == V and VP <= P and V <= 2048 and D == P and UNITS % 2 == 0 and NR % 2 == 1
    assert NV % 2 == 1 and MC * PC == NV and KP <= P and HI * NV <= 512
    w1_pieces = pair_weight_pieces(NV, HALF, MC)
    SHUFFLED = 16 * NJ * PC
    WEIGHTS = 16 * (len(w1_pieces) + 5)
    dots = nc.dram_tensor("dots", (2, NJ, NI * WIDE * Q // NJ), F32, kind="Internal").ap()

    with ExitStack() as ctx:
        def sb(name, shape, dt):
            return ctx.enter_context(nc.sbuf_tensor(name, shape, dt))

        def psum(name, shape, dt):
            return ctx.enter_context(nc.psum_tensor(name, shape, dt))

        def sem(name):
            return ctx.enter_context(nc.semaphore(name))

        T = sb("T", [P, 2, Q, NV], F32)
        tab_hi = sb("tab_hi", [P, ONEHOT, CH, D], F32R)
        tab_lo = sb("tab_lo", [P, ONEHOT, CH, D], F32R)
        hot = sb("hot", [P, 2, CH, Q], F32R)
        rows = sb("rows", [P, 2, len(flat), D], F32)
        gram = sb("gram", [P, NV, Q // NJ], F32)
        pairs = sb("pairs", [P, 2, PC, Q], F32)
        w1 = sb("w1", [P, PC + 1, F1], F32)
        w2 = sb("w2", [P, F1C, F2], F32)
        w3 = sb("w3", [P, F2C], F32)
        bias1 = sb("bias1", [P, F1C], F32)
        bias2 = sb("bias2", [P, F2C], F32)
        h1 = sb("h1", [P, F1C, Q], F32)
        h2 = sb("h2", [P, F2C, 2, P], F32)
        y = sb("y", [P, TILES], F32)
        ids_all = sb("ids_all", [P, TILES, NT], I32)
        ids_hot = sb("ids_hot", [P, ONEHOT * (TILES - 1) + P], F32)
        ids_t = sb("ids_t", [P, UNITS + 1, Q], F16)
        idx = sb("idx", [P, 4, NT], I32)
        ident = sb("ident", [P, P], F32)
        row_no = sb("row_no", [P, CH], F32)
        pick = sb("pick", [P, ONEHOT, P], F16)
        stage = T[:, 1].rearrange("p q n -> p (q n)")
        raw = [stage[:VP, i * CH * D:(i + 1) * CH * D] for i in range(RAWS)]
        top = [stage[:VP, (RAWS + i) * CH * D:(RAWS + i + 1) * CH * D] for i in range(2)]
        look_ps = psum("look_ps", [P, 2, 512], F32)
        ids_ps = psum("ids_ps", [P, 2, 512], F32)
        gram_ps = psum("gram_ps", [P, 2, 512], F32)
        mlp_ps = psum("mlp_ps", [P, 2, 2, Q], F32)

        idx_landed = [sem(f"idx_landed{i}") for i in range(4)]
        dense_landed = [sem(f"dense_landed{i}") for i in range(2)]
        rows_landed = [[sem(f"rows_landed{i}_{r}") for r in range(NR)] for i in range(2)]
        ids_landed = sem("ids_landed")
        raw_landed = [sem(f"raw_landed{i}") for i in range(RAWS)]
        weights_landed = sem("weights_landed")
        dots_stored = sem("dots_stored")
        shuffled = [sem(f"shuffled{i}") for i in range(2)]
        stored = sem("stored")
        tiles_begun = sem("tiles_begun")
        ident_zero = sem("ident_zero")
        ident_ready = sem("ident_ready")
        pick_zero = sem("pick_zero")
        pick_ready = sem("pick_ready")
        row_no_ready = sem("row_no_ready")
        ids_hot_ready = sem("ids_hot_ready")
        ids_t_zero = sem("ids_t_zero")
        ids_turned = sem("ids_turned")
        ids_t_ready = sem("ids_t_ready")
        top_ready = sem("top_ready")
        hi_ready = sem("hi_ready")
        lo_ready = sem("lo_ready")
        ids_spread = sem("ids_spread")
        hot_ready = sem("hot_ready")
        hot_looked = sem("hot_looked")
        turned = sem("turned")
        look_free = sem("look_free")
        gram_done = sem("gram_done")
        gram_free = sem("gram_free")
        l1_done = sem("l1_done")
        h1_ready = sem("h1_ready")
        l2_done = sem("l2_done")
        h2_ready = sem("h2_ready")
        l3_done = sem("l3_done")
        y_ready = sem("y_ready")

        ids_v = ids.rearrange("(p t) f -> p t f", p=P)
        dense_v = r_dense.rearrange("(p t) d -> p t d", p=P)
        T_tile = [[T[:, par].rearrange("p (j l i) n -> p l n j i", j=NJ, l=2)[:, l] for l in range(2)]
                  for par in range(2)]
        QJ = Q // NJ

        def tile_of(it, a, l):
            return 4 * it + 2 * a + l

        def ids_bank(u):
            banks = [mlp_ps[:, 0].rearrange("p f q -> p (f q)"), mlp_ps[:, 1].rearrange("p f q -> p (f q)"),
                     look_ps[:, 0], look_ps[:, 1]]
            return banks[u // 2][:, u % 2 * Q:(u % 2 + 1) * Q]

        turns = [[("turn", l, r) for r in range(NR)] for l in range(2)]
        looks = [("look", k) for k in range(ONEHOT)]
        EARLY = ONEHOT // 2
        STEP0 = ONEHOT // 2 + 1
        START = looks[:EARLY] + turns[0] + looks[EARLY:]
        FIRST = looks[:STEP0] + turns[1][:2] + [looks[STEP0]] + turns[1][2:4] + [looks[STEP0 + 1]] + turns[1][4:] \
            + looks[STEP0 + 2:]
        ORDER = turns[0][:2] + [looks[0]] + turns[0][2:4] + [looks[1]] + turns[0][4:] + looks[2:STEP0] \
            + FIRST[STEP0:]
        LAST = turns[0] + turns[1]
        assert len(START) + len(FIRST) == ONEHOT + len(ORDER) and len(ORDER) % 2 == 0 and ONEHOT % 2 == 0

        def use_of(it, a, key, order):
            if order is START:
                return START.index(key)
            if order is FIRST:
                return len(START) + FIRST.index(key)
            return ONEHOT + len(ORDER) * (2 * it + a) + order.index(key)

        def bank_of(key, order):
            return use_of(0, 0, key, order) % 2

        block = ctx.enter_context(nc.Block())

        @block.sync
        def _(sp):
            def load_idx(it, a, l):
                t, s = tile_of(it, a, l), (2 * a + l) % 4
                sp.dma_start(idx[:, s, :], ids_v[:, bass.ds(t, 1), :].rearrange("p a f -> p (a f)")
                             ).then_inc(idx_landed[s], 16)

            def load_dense(it, a, l):
                t = tile_of(it, a, l)
                sp.dma_start(rows[:, l, place[0], :], dense_v[:, bass.ds(t, 1), :].rearrange("p a d -> p (a d)")
                             ).then_inc(dense_landed[l], 16)

            def load_raw(k):
                if k >= RAWS:
                    sp.wait_ge(lo_ready, k - RAWS + 1)
                sp.dma_start(raw[k % RAWS], tables[onehot[k]].rearrange("(p c) d -> p (c d)", c=CH)
                             ).then_inc(raw_landed[k % RAWS], 16)

            def load_weights():
                for w_row, cnt, c, r, step in w1_pieces:
                    sp.dma_start(w1[r:r + step * (cnt - 1) + 1:step, c, :], W1[w_row:w_row + cnt, :]
                                 ).then_inc(weights_landed, 16)
                sp.dma_start(w1[:, PC, :], W1[PAIRS:PAIRS + D, :]).then_inc(weights_landed, 16)
                sp.dma_start(w2[:], W2.rearrange("(c p) f -> p c f", p=P)).then_inc(weights_landed, 16)
                with nc.allow_non_contiguous_dma(reason="a few hundred words"):
                    sp.dma_start(w3[:], W3.rearrange("(c p) o -> p (c o)", p=P)).then_inc(weights_landed, 16)
                    sp.dma_start(bias1[:], b1.rearrange("(c p) -> p c", p=P)).then_inc(weights_landed, 16)
                    sp.dma_start(bias2[:], b2.rearrange("(c p) -> p c", p=P)).then_inc(weights_landed, 16)

            def unit(it, a, last=False):
                if not last:
                    load_idx(it, a + 1, 0)
                for l in range(2):
                    if not last:
                        sp.wait_ge(turned, 2 * NR + NR * (tile_of(it, a, l) + 1))
                        load_dense(it, a + 1, l)
                        if l == 0:
                            load_idx(it, a + 1, 1)
                sp.wait_ge(gram_free, 2 + 4 * (2 * it + a + 1))
                rows_v = dots[a % 2].rearrange("j (m n i) -> (j m) n i", m=NI, n=WIDE)
                sp.dma_start(rows_v[:, 0:NV, :], gram[:]).then_inc(dots_stored, 16)
                sp.dma_start(rows_v[:, NV:WIDE, :], gram[:, 0:HALF]).then_inc(dots_stored, 16)
                sp.wait_ge(dots_stored, 32 * (2 * it + a + 1))
                for c in range(PC):
                    first, step = MC * c * WIDE + MC * c + 1, WIDE + 1
                    for j in range(NJ):
                        src = dots[a % 2, j, first * QJ:(first + MC * step) * QJ].rearrange("(m x) -> m x", m=MC)
                        sp.dma_start(pairs[0:KP, a % 2, c, j * QJ:(j + 1) * QJ],
                                     src[:, 0:HALF * QJ].rearrange("m (k i) -> m k i", i=QJ)
                                     ).then_inc(shuffled[a % 2], 16)

            load_idx(0, 0, 0)
            sp.dma_start(ids_all[:], ids_v).then_inc(ids_landed, 16)
            load_raw(0)
            load_raw(1)
            load_idx(0, 0, 1)
            load_dense(0, 0, 0)
            load_dense(0, 0, 1)
            for k in range(2, ONEHOT):
                load_raw(k)
            load_weights()
            unit(0, 0)
            with sp.Fori(0, UNITS // 2 - 1) as it:
                unit(it, 1)
                unit(it, 2)
            unit(UNITS // 2 - 1, 1, last=True)
            sp.wait_ge(y_ready, UNITS)
            sp.dma_start(out.rearrange("(p t) o -> p (t o)", p=P), y[:]).then_inc(stored, 16)
            sp.wait_ge(stored, 16)

        @block.gpsimd
        def _(pool):
            nc.gpsimd.memset(ident[:], 0.0).then_inc(ident_zero, 1)
            pool.wait_ge(ident_zero, 1)
            nc.gpsimd.affine_select(out=ident[:], in_=ident[:], compare_op=ALU.not_equal, fill=1.0, base=0,
                                    pattern=[[-1, P]], channel_multiplier=1).then_inc(ident_ready, 1)
            nc.gpsimd.iota(row_no[:], pattern=[[1, CH]], base=0, channel_multiplier=CH,
                           allow_small_or_imprecise_dtypes=True).then_inc(row_no_ready, 1)
            pool.wait_ge(pick_zero, 1)
            nc.gpsimd.affine_select(out=pick[:], in_=pick[:], compare_op=ALU.not_equal, fill=1.0, base=0,
                                    pattern=[[-1, ONEHOT], [0, P]], channel_multiplier=1).then_inc(pick_ready, 1)

            def gather(it, a, l):
                t, s = tile_of(it, a, l), (2 * a + l) % 4
                pool.wait_ge(idx_landed[s], 16 * (it + (2 * a + l) // 4 + 1))
                pool.wait_ge(turned, NR * (t + 1))
                pool.sem_inc(tiles_begun, 1)
                for r in range(NR):
                    for n in rounds[r]:
                        if n == 0:
                            continue
                        pool.indirect_dma_start(
                            rows[:, l, place[n], :], None, tables[n - 1],
                            bass.IndirectOffsetOnAxis(ap=idx[:, s, n - 1:n].bitcast(U32), axis=0),
                        ).then_inc(rows_landed[l][r], 16)

            with pool.Fori(0, UNITS // 2) as it:
                for a in range(2):
                    for l in range(2):
                        gather(it, a, l)

        @block.vector
        def _(dve):
            nc.vector.memset(pick[:], 0.0).then_inc(pick_zero, 1)
            for h in range(2):
                nc.vector.memset(gram_ps[:, h, :], 0.0).then_inc(gram_free, 1)
            nc.vector.memset(ids_t[:], 0.0).then_inc(ids_t_zero, 1)
            nc.vector.memset(ids_hot[:, ONEHOT * TILES:], 0.0).then_inc(ids_hot_ready, 1)
            dve.wait_ge(ids_landed, 16)
            ids_hot_v = ids_hot[:, 0:ONEHOT * TILES].rearrange("p (t k) -> p t k", k=ONEHOT)
            nc.vector.tensor_copy(ids_hot_v[:, :, 0:1], ids_all[:, :, onehot[0]:onehot[0] + 1]).then_inc(ids_hot_ready, 1)
            nc.vector.tensor_copy(ids_hot_v[:, :, 1:], ids_all[:, :, onehot[1]:onehot[-1] + 1]).then_inc(ids_hot_ready, 1)

            def split(k):
                dve.wait_ge(raw_landed[k % RAWS], 16 * (k // RAWS + 1))
                if k >= 2:
                    dve.wait_ge(hi_ready, k - 1)
                nc.vector.tensor_scalar(top[k % 2].bitcast(I32), raw[k % RAWS].bitcast(I32), -(1 << LOW_BITS), None,
                                        ALU.bitwise_and).then_inc(top_ready, 1)
                dve.wait_ge(top_ready, k + 1)
                nc.vector.tensor_tensor(tab_lo[:VP, k].rearrange("p c d -> p (c d)"), raw[k % RAWS], top[k % 2],
                                        ALU.subtract).then_inc(lo_ready, 1)

            def compare(g, k):
                dve.wait_ge(ids_spread, g + 1)
                if not (isinstance(g, int) and g < 2):
                    dve.wait_ge(hot_looked, g - 1)
                nc.vector.tensor_tensor(
                    hot[:VP, k % 2], ids_ps[:VP, k % 2, 0:Q].unsqueeze(1).to_broadcast([VP, CH, Q]),
                    row_no[:VP, :].unsqueeze(2).to_broadcast([VP, CH, Q]), ALU.is_equal).then_inc(hot_ready, 1)

            def gram_out(it, a, l):
                if l == 0 and not (isinstance(it, int) and (it, a) == (0, 0)):
                    dve.wait_ge(dots_stored, 32 * (2 * it + a))
                for h in range(2):
                    dve.wait_ge(gram_done, 2 * tile_of(it, a, l) + h + 1)
                    i0 = l * NI + h * HI
                    nc.vector.tensor_copy(
                        gram[:, :, i0:i0 + HI],
                        gram_ps[:, h, 0:HI * NV].rearrange("p (i n) -> p n i", n=NV)).then_inc(gram_free, 1)

            def unit(it, a, last=False):
                g = ONEHOT * (2 * it + a + 1)
                if not last:
                    for k in range(2, STEP0):
                        compare(g + k, k)
                gram_out(it, a, 0)
                if not last:
                    for k in range(STEP0, ONEHOT + 2):
                        compare(g + k, k)
                gram_out(it, a, 1)

            split(0)
            split(1)
            dve.wait_ge(row_no_ready, 1)
            compare(0, 0)
            compare(1, 1)
            for k in range(2, ONEHOT):
                split(k)
                compare(k, k)
            compare(ONEHOT, 0)
            compare(ONEHOT + 1, 1)
            unit(0, 0)
            with dve.Fori(0, UNITS // 2 - 1) as it:
                unit(it, 1)
                unit(it, 2)
            unit(UNITS // 2 - 1, 1, last=True)

        @block.scalar
        def _(act):
            nc.scalar.nop().then_inc(look_free, 2)
            act.wait_ge(ids_t_zero, 1)
            ids_t_v = ids_t[:].rearrange("p u (j l i) -> p u l j i", j=NJ, l=2)
            for u in range(UNITS):
                act.wait_ge(ids_turned, u // 2 + 1)
                nc.scalar.copy(ids_t_v[0:ONEHOT, u], ids_bank(u)[0:ONEHOT].rearrange("p (l j i) -> p l j i", l=2, j=NJ)
                               ).then_inc(ids_t_ready, 1)

            def hi_out(k):
                act.wait_ge(top_ready, k + 1)
                nc.scalar.copy(tab_hi[:VP, k].rearrange("p c d -> p (c d)"), top[k % 2]).then_inc(hi_ready, 1)

            def hot_out(it, a, k, order):
                act.wait_ge(hot_looked, ONEHOT * (2 * it + a) + k + 1)
                nc.scalar.copy(T[:, a % 2, :, onehot[k] + 1], look_ps[:, bank_of(("look", k), order), 0:Q]
                               ).then_inc(look_free, 1)

            def turn_out(it, a, l, first_round, end_round, order):
                for r in range(first_round, end_round):
                    n, cnt = rounds[r][0], len(rounds[r])
                    act.wait_ge(turned, 2 * NR + NR * tile_of(it, a, l) + r + 1)
                    nc.scalar.copy(T_tile[a % 2][l][:, n:n + cnt],
                                   look_ps[:, bank_of(("turn", l, r), order), 0:cnt * P].rearrange(
                                       "p (n j i) -> p n j i", n=cnt, j=NJ)).then_inc(look_free, 1)

            def h1_out(it, a):
                act.wait_ge(weights_landed, WEIGHTS)
                for f in range(F1C):
                    act.wait_ge(l1_done, F1C // 2 * (2 * it + a) + f // 2 + 1)
                    nc.scalar.activation(h1[:, f], mlp_ps[:, f // 2, f % 2], ACT.Relu, bias=bias1[:, f:f + 1]
                                         ).then_inc(h1_ready, 1)

            def h2_out(it, a):
                act.wait_ge(l2_done, 2 * it + a + 1)
                for f in range(F2C):
                    nc.scalar.activation(h2[:, f].rearrange("p l (j i) -> p j l i", j=NJ),
                                         mlp_ps[:, 0, f].rearrange("p (j l i) -> p j l i", j=NJ, l=2),
                                         ACT.Relu, bias=bias2[:, f:f + 1]
                                         ).then_inc(h2_ready, 1)

            def y_out(it, a):
                act.wait_ge(l3_done, 2 * it + a + 1)
                nc.scalar.copy(y[:, bass.ds(tile_of(it, a, 0), 2)], mlp_ps[:, 1, 0, 0:2]).then_inc(y_ready, 1)

            def unit(it, a, order):
                if order is ORDER:
                    turn_out(it, a, 0, 0, 2, order)
                    hot_out(it, a + 1, 0, order)
                    turn_out(it, a, 0, 2, 4, order)
                    hot_out(it, a + 1, 1, order)
                    turn_out(it, a, 0, 4, NR, order)
                for k in range(2 if order is ORDER else 0, STEP0):
                    hot_out(it, a + 1, k, order)
                turn_out(it, a, 1, 0, 2, order)
                hot_out(it, a + 1, STEP0, order)
                turn_out(it, a, 1, 2, 4, order)
                hot_out(it, a + 1, STEP0 + 1, order)
                turn_out(it, a, 1, 4, NR, order)
                if order is ORDER:
                    h1_out(it, a - 1)
                for k in range(STEP0 + 2, ONEHOT):
                    hot_out(it, a + 1, k, order)
                if order is ORDER:
                    h2_out(it, a - 1)
                    y_out(it, a - 1)

            for k in range(ONEHOT):
                hi_out(k)
                if k >= 1:
                    hot_out(0, 0, k - 1, START)
                if k == EARLY:
                    turn_out(0, 0, 0, 0, NR, START)
            hot_out(0, 0, ONEHOT - 1, START)
            unit(0, 0, FIRST)
            with act.Fori(0, UNITS // 2 - 1) as it:
                unit(it, 1, ORDER)
                unit(it, 2, ORDER)
            end = UNITS // 2 - 1
            for l in range(2):
                turn_out(end, 1, l, 0, NR, LAST)
            h1_out(end, 0)
            h2_out(end, 0)
            y_out(end, 0)
            h1_out(end, 1)
            h2_out(end, 1)
            y_out(end, 1)

        @block.tensor
        def _(pe):
            nc.tensor.nop().then_inc(turned, 2 * NR)

            def spread(it, a, k):
                pe.matmul(ids_ps[:, k % 2, 0:Q], pick[:, k], ids_t[:, unit_no(it, a)], start=True, stop=True
                          ).then_inc(ids_spread, 1)

            def unit_no(it, a):
                return 2 * it + a

            def lookup(it, a, k, order, users):
                g = ONEHOT * (2 * it + a) + k
                pe.wait_ge(hot_ready, g + 1)
                if k + 2 < ONEHOT:
                    spread(it, a, k + 2)
                else:
                    spread(it, a + 1, k + 2 - ONEHOT)
                if order is START:
                    pe.wait_ge(hi_ready, k + 1)
                    pe.wait_ge(lo_ready, k + 1)
                pe.wait_ge(look_free, use_of(*users, ("look", k), order) + 1)
                for c in range(CH):
                    for half, w in enumerate((tab_hi, tab_lo)):
                        mm = pe.matmul(look_ps[:, bank_of(("look", k), order), 0:Q], w[:VP, k, c], hot[:VP, k % 2, c],
                                       start=(c == 0 and half == 0), stop=(c == CH - 1 and half == 1))
                mm.then_inc(hot_looked, 1)

            def turn(it, a, l, first_round, end_round, order):
                use = 2 * it + a + 1
                for r in range(first_round, end_round):
                    if 0 in rounds[r]:
                        pe.wait_ge(dense_landed[l], 16 * use)
                    pe.wait_ge(rows_landed[l][r], 16 * (len(rounds[r]) - (0 in rounds[r])) * use)
                    pe.wait_ge(look_free, use_of(it, a, ("turn", l, r), order) + 1)
                    bank = bank_of(("turn", l, r), order)
                    for i, n in enumerate(rounds[r]):
                        mm = pe.transpose(look_ps[:, bank, i * P:(i + 1) * P], rows[:, l, place[n], :], ident[:])
                    mm.then_inc(turned, 1)

            def products(it, a, l, last_use, order):
                t = tile_of(it, a, l)
                pe.wait_ge(look_free, 2 + use_of(it, a, last_use, order) + 1)
                for h in range(2):
                    pe.wait_ge(gram_free, 2 * t + h + 1)
                    for i in range(HI):
                        for j in range(NJ):
                            q = (j * 2 + l) * NI + h * HI + i
                            mm = pe.matmul(gram_ps[32 * j:32 * j + NV, h, i * NV:(i + 1) * NV],
                                           T[:, a % 2, q, :], T[:, a % 2, q, 0:NV], start=True, stop=True)
                    mm.then_inc(gram_done, 1)

            def layer1(it, a):
                pe.wait_ge(weights_landed, WEIGHTS)
                pe.wait_ge(shuffled[a % 2], SHUFFLED * (it + a // 2 + 1))
                for f in range(F1C):
                    for c in range(PC + 1):
                        kk = P if c == PC else KP
                        rhs = T[:, a % 2, :, 0] if c == PC else pairs[:kk, a % 2, c]
                        mm = pe.matmul(mlp_ps[:, f // 2, f % 2], w1[:kk, c, f * P:(f + 1) * P], rhs,
                                       start=(c == 0), stop=(c == PC))
                    if f % 2:
                        mm.then_inc(l1_done, 1)

            def layer2(it, a):
                for f in range(F2C):
                    for c in range(F1C):
                        if f == 0:
                            pe.wait_ge(h1_ready, F1C * (2 * it + a) + (c + 1 if c >= 2 else 2))
                        mm = pe.matmul(mlp_ps[:, 0, f], w2[:, c, f * P:(f + 1) * P], h1[:, c],
                                       start=(c == 0), stop=(c == F1C - 1))
                mm.then_inc(l2_done, 1)

            def layer3(it, a):
                pe.wait_ge(h2_ready, F2C * (2 * it + a + 1))
                for l in range(2):
                    for c in range(F2C):
                        mm = pe.matmul(mlp_ps[:, 1, 0, l:l + 1], h2[:, c, l], w3[:, c:c + 1],
                                       start=(c == 0), stop=(c == F2C - 1))
                mm.then_inc(l3_done, 1)

            def unit(it, a, order):
                def look(k):
                    lookup(it, a + 1, k, order, (it, a))

                if order is ORDER:
                    turn(it, a, 0, 0, 2, order)
                    look(0)
                    turn(it, a, 0, 2, 4, order)
                    look(1)
                    turn(it, a, 0, 4, NR, order)
                    look(2)
                    products(it, a, 0, turns[0][-1], order)
                else:
                    products(it, a, 0, START[-1], START)
                    for k in range(3):
                        look(k)
                for k in range(3, STEP0):
                    look(k)
                turn(it, a, 1, 0, 2, order)
                look(STEP0)
                turn(it, a, 1, 2, 4, order)
                look(STEP0 + 1)
                turn(it, a, 1, 4, NR, order)
                if order is ORDER:
                    layer1(it, a - 1)
                for k in range(STEP0 + 2, ONEHOT):
                    look(k)
                if order is ORDER:
                    layer2(it, a - 1)
                products(it, a, 1, turns[1][-1], order)
                if order is ORDER:
                    layer3(it, a - 1)

            pe.wait_ge(ident_ready, 1)
            pe.wait_ge(ids_hot_ready, 3)
            for t in range(TILES):
                mm = pe.transpose(ids_bank(t // 2)[:, (t % 2) * P:(t % 2 + 1) * P],
                                  ids_hot[:, t * ONEHOT:t * ONEHOT + P], ident[:])
                if t % 4 == 3:
                    mm.then_inc(ids_turned, 1)
            pe.wait_ge(pick_ready, 1)
            pe.wait_ge(ids_t_ready, UNITS)
            spread(0, 0, 0)
            spread(0, 0, 1)
            for k in range(ONEHOT):
                if k == EARLY:
                    turn(0, 0, 0, 0, NR, START)
                lookup(0, 0, k, START, (0, 0))
            unit(0, 0, FIRST)
            with pe.Fori(0, UNITS // 2 - 1) as it:
                unit(it, 1, ORDER)
                unit(it, 2, ORDER)
            end = UNITS // 2 - 1
            for l in range(2):
                turn(end, 1, l, 0, NR, LAST)
                products(end, 1, l, turns[l][-1], LAST)
            for a in range(2):
                if a == 1:
                    pe.wait_ge(y_ready, UNITS - 1)
                layer1(end, a)
                layer2(end, a)
                layer3(end, a)


_INS = ['r_dense', 'ids'] + [f'tbl_{i}' for i in range(26)] + ['W_top1', 'b_top1', 'W_top2', 'b_top2', 'W_top3']


def kernel(**inputs):
    import numpy as _np
    import concourse.bacc as _bacc
    from concourse import mybir as _mybir
    from concourse.bass_utils import run_bass_kernel_spmd as _run

    nc = _bacc.Bacc("TRN2", target_bir_lowering=False, num_devices=1)
    arrays, args = {}, []
    for name in _INS:
        a = _np.ascontiguousarray(inputs[name])
        arrays[f"in_{name}_dram"] = a
        args.append(nc.dram_tensor(f"in_{name}_dram", a.shape, _mybir.dt.from_np(a.dtype), kind="ExternalInput").ap())
    out = nc.dram_tensor("out_0_dram", (inputs['r_dense'].shape[0], 1), _mybir.dt.float32, kind="ExternalOutput").ap()
    dlrm_tower(nc, args[0], args[1], args[2:28], *args[28:33], out)
    r = _run(nc, [arrays], core_ids=[0])
    return r.results[0]["out_0_dram"]
```

```python
from contextlib import ExitStack

import concourse.bass as bass
from concourse import mybir

F32 = mybir.dt.float32
F32R = mybir.dt.float32r
F16 = mybir.dt.float16
I32 = mybir.dt.int32
U32 = mybir.dt.uint32
ALU = mybir.AluOpType
ACT = mybir.ActivationFunctionType

P = 128
ONEHOT = 8
RING = 4
RAWS = 4
MAX_ROUND = 4
LOW_BITS = 12


def plan(table_rows):
    nt = len(table_rows)
    least = min(table_rows)
    small = [f for f in range(nt) if table_rows[f] == least]
    onehot = sorted(small[-(ONEHOT - 1):] + small[:1])
    runs = []
    for n in range(nt + 1):
        if n - 1 in onehot:
            continue
        if runs and runs[-1][-1] == n - 1 and len(runs[-1]) < MAX_ROUND:
            runs[-1].append(n)
        else:
            runs.append([n])
    return onehot, runs


def pair_weight_pieces(nv, half, per_chunk):
    def triu(n, m):
        return n * nv - n * (n + 1) // 2 + m - n - 1

    pieces = []
    for m in range(nv - 1):
        pieces.append((triu(m, m + 1), min(half, nv - 1 - m), m // per_chunk, m % per_chunk * half, 1))
    for n in range(half):
        m = nv - half + n
        while m < nv:
            cnt = min(nv - m, per_chunk - m % per_chunk)
            pieces.append((triu(n, m), cnt, m // per_chunk, m % per_chunk * half + n + nv - m - 1, half - 1))
            m += cnt
    return pieces


def dlrm_tower(nc, r_dense, ids, tables, W1, b1, W2, b2, W3, out):
    B, NT = ids.shape
    D = r_dense.shape[1]
    F1, F2 = W1.shape[1], W2.shape[1]
    NV = NT + 1
    HALF = (NV - 1) // 2
    PAIRS = NV * HALF
    TILES = B // P
    UNITS = TILES // 2
    Q = 2 * P
    NJ, NI = 4, P // 4
    HI = NI // 2
    F1C, F2C = F1 // P, F2 // P
    PC = -(-PAIRS // P)
    MC = NV // PC
    KP = MC * HALF
    WIDE = NV + HALF
    onehot, rounds = plan([t.shape[0] for t in tables])
    NR = len(rounds)
    flat = [n for r in rounds for n in r]
    place = {n: i for i, n in enumerate(flat)}
    V = tables[onehot[0]].shape[0]
    CH = 8
    VP = V // CH
    assert VP * CH == V and VP <= P and V <= 2048 and D == P and UNITS % 2 == 0 and NR % 2 == 1
    assert NV % 2 == 1 and MC * PC == NV and KP <= P and HI * NV <= 512
    w1_pieces = pair_weight_pieces(NV, HALF, MC)
    SHUFFLED = 16 * NJ * PC
    SHUFFLED_LAST = 16 * PC
    WEIGHTS = 16 * (len(w1_pieces) + 5)
    dots = nc.dram_tensor("dots", (2, NJ, NI * WIDE * Q // NJ), F32, kind="Internal").ap()
    ids_rows = nc.dram_tensor("ids_rows", (UNITS, ONEHOT, Q), F16, kind="Internal").ap()
    dots_last = nc.dram_tensor("dots_last", (2, NV + 1, WIDE, P), F32, kind="Internal").ap()

    with ExitStack() as ctx:
        def sb(name, shape, dt):
            return ctx.enter_context(nc.sbuf_tensor(name, shape, dt))

        def psum(name, shape, dt):
            return ctx.enter_context(nc.psum_tensor(name, shape, dt))

        def sem(name):
            return ctx.enter_context(nc.semaphore(name))

        T = sb("T", [P, 2, Q, NV], F32)
        tab_hi = sb("tab_hi", [P, ONEHOT, CH, D], F32R)
        tab_lo = sb("tab_lo", [P, ONEHOT, CH, D], F32R)
        hot = sb("hot", [P, 2, CH, Q], F32R)
        rows = sb("rows", [P, 2, len(flat), D], F32)
        gram = sb("gram", [P, NV, Q // NJ], F32)
        pairs = sb("pairs", [P, 2, PC, Q], F32)
        w1 = sb("w1", [P, PC + 1, F1], F32)
        w2 = sb("w2", [P, F1C, F2], F32)
        w3 = sb("w3", [P, F2C], F32)
        bias1 = sb("bias1", [P, F1C], F32)
        bias2 = sb("bias2", [P, F2C], F32)
        h1 = sb("h1", [P, F1C, Q], F32)
        h2 = sb("h2", [P, F2C, 2, P], F32)
        y = sb("y", [P, TILES], F32)
        ids_all = sb("ids_all", [P, TILES, NT], I32)
        ids_hot = sb("ids_hot", [P, ONEHOT * (TILES - 1) + P], F32)
        ids_near = sb("ids_near", [P, 2, ONEHOT, Q], F16)
        idx = sb("idx", [P, 4, NT], I32)
        ident = sb("ident", [P, P], F32)
        minus_row = sb("minus_row", [P, 1], F32)
        stage = T[:, 1].rearrange("p q n -> p (q n)")
        raw = [stage[:VP, i * CH * D:(i + 1) * CH * D] for i in range(RAWS)]
        top = [stage[:VP, (RAWS + i) * CH * D:(RAWS + i + 1) * CH * D] for i in range(2)]
        ids_t = pairs[:].rearrange("p a c q -> p (a c q)").bitcast(F16)[0:ONEHOT, 0:UNITS * Q].rearrange(
            "p (u q) -> p u q", u=UNITS)
        gram_last = [rows[:, l].rearrange("p n d -> p (n d)")[:, 0:WIDE * NI].rearrange(
            "p (n i) -> p n i", n=WIDE) for l in range(2)]
        look_ps = psum("look_ps", [P, RING, 512], F32)
        gram_ps = psum("gram_ps", [P, 2, 512], F32)
        mlp_ps = psum("mlp_ps", [P, 2, 2, Q], F32)

        idx_landed = [sem(f"idx_landed{i}") for i in range(4)]
        dense_landed = [sem(f"dense_landed{i}") for i in range(2)]
        rows_landed = [[sem(f"rows_landed{i}_{r}") for r in range(NR)] for i in range(2)]
        ids_landed = sem("ids_landed")
        ids_rows_stored = sem("ids_rows_stored")
        ids_near_landed = [sem(f"ids_near_landed{i}") for i in range(2)]
        raw_landed = [sem(f"raw_landed{i}") for i in range(RAWS)]
        weights_landed = sem("weights_landed")
        dots_stored = sem("dots_stored")
        shuffled = [sem(f"shuffled{i}") for i in range(2)]
        dots_last_stored = [sem(f"dots_last_stored{l}") for l in range(2)]
        shuffled_last = [sem(f"shuffled_last{l}") for l in range(2)]
        stored = sem("stored")
        tiles_begun = sem("tiles_begun")
        ident_zero = sem("ident_zero")
        ident_ready = sem("ident_ready")
        minus_row_ready = sem("minus_row_ready")
        ids_relative = sem("ids_relative")
        ids_hot_ready = sem("ids_hot_ready")
        ids_turned = sem("ids_turned")
        ids_t_ready = sem("ids_t_ready")
        top_ready = sem("top_ready")
        hi_ready = sem("hi_ready")
        lo_ready = sem("lo_ready")
        hot_ready = sem("hot_ready")
        hot_looked = sem("hot_looked")
        turned = sem("turned")
        look_free = sem("look_free")
        gram_done = sem("gram_done")
        gram_free = sem("gram_free")
        l1_done = sem("l1_done")
        h1_ready = sem("h1_ready")
        l2_done = sem("l2_done")
        h2_ready = sem("h2_ready")
        l3_done = sem("l3_done")
        y_ready = sem("y_ready")

        ids_v = ids.rearrange("(p t) f -> p t f", p=P)
        dense_v = r_dense.rearrange("(p t) d -> p t d", p=P)
        T_tile = [[T[:, par].rearrange("p (j l i) n -> p l n j i", j=NJ, l=2)[:, l] for l in range(2)]
                  for par in range(2)]
        QJ = Q // NJ

        def tile_of(it, a, l):
            return 4 * it + 2 * a + l

        def ids_bank(u):
            banks = [mlp_ps[:, 0].rearrange("p f q -> p (f q)"), mlp_ps[:, 1].rearrange("p f q -> p (f q)"),
                     look_ps[:, 0], look_ps[:, 1]]
            return banks[u // 2][:, u % 2 * Q:(u % 2 + 1) * Q]

        turns = [[("turn", l, r) for r in range(NR)] for l in range(2)]
        looks = [("look", k) for k in range(ONEHOT)]
        EARLY = ONEHOT // 2
        START = looks[:EARLY] + turns[0] + looks[EARLY:]
        SECOND = [turns[1][0], looks[NR], turns[1][1], turns[1][2], *looks[NR + 1:ONEHOT - 1], *turns[1][3:],
                  looks[ONEHOT - 1]]
        FIRST = turns[1] + looks
        ORDER = [key for r in range(NR) for key in (turns[0][r], looks[r])] + SECOND
        LAST = turns[0] + turns[1]
        assert len(START) + len(FIRST) == ONEHOT + len(ORDER) and 2 * len(ORDER) % RING == 0 and ONEHOT % 2 == 0

        def use_of(it, a, key, order):
            if order is START:
                return START.index(key)
            if order is FIRST:
                return len(START) + FIRST.index(key)
            return ONEHOT + len(ORDER) * (2 * it + a) + order.index(key)

        def bank_of(a, key, order):
            return use_of(0, a, key, order) % RING

        def last_l1(l, f):
            bank = (mlp_ps[:, f // 2].rearrange("p f q -> p (f q)") if l == 1 else look_ps[:, f // 2])
            return bank[:, f % 2 * P:(f % 2 + 1) * P]

        def last_l2(l, f):
            return look_ps[:, 2 + l, f * P:(f + 1) * P]

        def last_l3(l):
            return look_ps[:, l, 0:1]

        block = ctx.enter_context(nc.Block())

        @block.sync
        def _(sp):
            def load_idx(it, a, l):
                t, s = tile_of(it, a, l), (2 * a + l) % 4
                sp.dma_start(idx[:, s, :], ids_v[:, bass.ds(t, 1), :].rearrange("p a f -> p (a f)")
                             ).then_inc(idx_landed[s], 16)

            def load_dense(it, a, l):
                t = tile_of(it, a, l)
                sp.dma_start(rows[:, l, place[0], :], dense_v[:, bass.ds(t, 1), :].rearrange("p a d -> p (a d)")
                             ).then_inc(dense_landed[l], 16)

            def load_raw(k):
                if k >= RAWS:
                    sp.wait_ge(lo_ready, k - RAWS + 1)
                sp.dma_start(raw[k % RAWS], tables[onehot[k]].rearrange("(p c) d -> p (c d)", c=CH)
                             ).then_inc(raw_landed[k % RAWS], 16)

            def load_weights():
                for w_row, cnt, c, r, step in w1_pieces:
                    sp.dma_start(w1[r:r + step * (cnt - 1) + 1:step, c, :], W1[w_row:w_row + cnt, :]
                                 ).then_inc(weights_landed, 16)
                sp.dma_start(w1[:, PC, :], W1[PAIRS:PAIRS + D, :]).then_inc(weights_landed, 16)
                sp.dma_start(w2[:], W2.rearrange("(c p) f -> p c f", p=P)).then_inc(weights_landed, 16)
                with nc.allow_non_contiguous_dma(reason="a few hundred words"):
                    sp.dma_start(w3[:], W3.rearrange("(c p) o -> p (c o)", p=P)).then_inc(weights_landed, 16)
                    sp.dma_start(bias1[:], b1.rearrange("(c p) -> p c", p=P)).then_inc(weights_landed, 16)
                    sp.dma_start(bias2[:], b2.rearrange("(c p) -> p c", p=P)).then_inc(weights_landed, 16)

            def load_ids_near(it, a):
                sp.dma_start(ids_near[:, a % 2], ids_rows[bass.ds(2 * it + a, 1)].rearrange("u k q -> u (k q)")
                             .to_broadcast([P, ONEHOT * Q])).then_inc(ids_near_landed[a % 2], 16)

            def unit(it, a, last=False, weights=False, ids_ahead=True):
                if not last:
                    load_idx(it, a + 1, 0)
                for l in range(2):
                    if not last:
                        sp.wait_ge(turned, 2 * NR + NR * (tile_of(it, a, l) + 1))
                        load_dense(it, a + 1, l)
                        if l == 0:
                            load_idx(it, a + 1, 1)
                    if l == 0 and ids_ahead:
                        sp.wait_ge(hot_ready, ONEHOT * (2 * it + a + 1))
                        load_ids_near(it, a + 2)
                    if l == 0 and weights:
                        load_weights()
                if last:
                    for l in range(2):
                        shuffle_last(l)
                    return
                sp.wait_ge(gram_free, 2 + 4 * (2 * it + a + 1))
                rows_v = dots[a % 2].rearrange("j (m n i) -> (j m) n i", m=NI, n=WIDE)
                sp.dma_start(rows_v[:, 0:NV, :], gram[:]).then_inc(dots_stored, 16)
                sp.dma_start(rows_v[:, NV:WIDE, :], gram[:, 0:HALF]).then_inc(dots_stored, 16)
                sp.wait_ge(dots_stored, 32 * (2 * it + a + 1))
                for c in range(PC):
                    first, step = MC * c * WIDE + MC * c + 1, WIDE + 1
                    for j in range(NJ):
                        src = dots[a % 2, j, first * QJ:(first + MC * step) * QJ].rearrange("(m x) -> m x", m=MC)
                        sp.dma_start(pairs[0:KP, a % 2, c, j * QJ:(j + 1) * QJ],
                                     src[:, 0:HALF * QJ].rearrange("m (k i) -> m k i", i=QJ)
                                     ).then_inc(shuffled[a % 2], 16)

            def shuffle_last(l):
                sp.wait_ge(gram_free, 2 + 2 * (TILES - 1 + l))
                dst = dots_last[l, 0:NV].rearrange("m n (j i) -> j m n i", j=NJ)
                for j in range(NJ):
                    sp.dma_start(dst[j], gram_last[l][32 * j:32 * j + NV]).then_inc(dots_last_stored[l], 16)
                sp.wait_ge(dots_last_stored[l], 16 * NJ)
                flat_dots = dots_last[l].rearrange("m n s -> (m n s)")
                for c in range(PC):
                    first, step = MC * c * WIDE + MC * c + 1, WIDE + 1
                    src = flat_dots[first * P:(first + MC * step) * P].rearrange("(m x) -> m x", m=MC)
                    sp.dma_start(pairs[0:KP, 1, c, l * P:(l + 1) * P],
                                 src[:, 0:HALF * P].rearrange("m (k s) -> m k s", s=P)
                                 ).then_inc(shuffled_last[l], 16)

            load_idx(0, 0, 0)
            sp.dma_start(ids_all[:], ids_v).then_inc(ids_landed, 16)
            for k in range(RAWS):
                load_raw(k)
            load_idx(0, 0, 1)
            sp.wait_ge(ids_t_ready, UNITS)
            sp.dma_start(ids_rows.rearrange("u k q -> k u q"), ids_t).then_inc(ids_rows_stored, 16)
            load_raw(RAWS)
            load_raw(RAWS + 1)
            sp.wait_ge(ids_rows_stored, 16)
            load_ids_near(0, 0)
            for k in range(RAWS + 2, ONEHOT):
                load_raw(k)
            load_dense(0, 0, 0)
            load_dense(0, 0, 1)
            load_ids_near(0, 1)
            unit(0, 0, weights=True)
            unit(0, 1)
            with sp.Fori(1, UNITS // 2 - 1) as it:
                unit(it, 0)
                unit(it, 1)
            unit(UNITS // 2 - 1, 0, ids_ahead=False)
            unit(UNITS // 2 - 1, 1, last=True, ids_ahead=False)
            sp.wait_ge(y_ready, UNITS + 1)
            sp.dma_start(out.rearrange("(p t) o -> p (t o)", p=P), y[:]).then_inc(stored, 16)
            sp.wait_ge(stored, 16)

        @block.gpsimd
        def _(pool):
            nc.gpsimd.memset(ident[:], 0.0).then_inc(ident_zero, 1)
            pool.wait_ge(ident_zero, 1)
            nc.gpsimd.affine_select(out=ident[:], in_=ident[:], compare_op=ALU.not_equal, fill=1.0, base=0,
                                    pattern=[[-1, P]], channel_multiplier=1).then_inc(ident_ready, 1)
            nc.gpsimd.iota(minus_row[:], pattern=[[0, 1]], base=0, channel_multiplier=-CH,
                           allow_small_or_imprecise_dtypes=True).then_inc(minus_row_ready, 1)
            def gather(it, a, l):
                t, s = tile_of(it, a, l), (2 * a + l) % 4
                pool.wait_ge(idx_landed[s], 16 * (it + (2 * a + l) // 4 + 1))
                pool.wait_ge(turned, NR * (t + 1))
                pool.sem_inc(tiles_begun, 1)
                for r in range(NR):
                    for n in rounds[r]:
                        if n == 0:
                            continue
                        pool.indirect_dma_start(
                            rows[:, l, place[n], :], None, tables[n - 1],
                            bass.IndirectOffsetOnAxis(ap=idx[:, s, n - 1:n].bitcast(U32), axis=0),
                        ).then_inc(rows_landed[l][r], 16)

            with pool.Fori(0, UNITS // 2) as it:
                for a in range(2):
                    for l in range(2):
                        gather(it, a, l)

        @block.vector
        def _(dve):
            nc.vector.memset(ids_hot[:, ONEHOT * TILES:], 0.0).then_inc(ids_hot_ready, 1)
            dve.wait_ge(ids_landed, 16)
            ids_hot_v = ids_hot[:, 0:ONEHOT * TILES].rearrange("p (t k) -> p t k", k=ONEHOT)
            nc.vector.tensor_copy(ids_hot_v[:, :, 0:1], ids_all[:, :, onehot[0]:onehot[0] + 1]).then_inc(ids_hot_ready, 1)
            nc.vector.tensor_copy(ids_hot_v[:, :, 1:], ids_all[:, :, onehot[1]:onehot[-1] + 1]).then_inc(ids_hot_ready, 1)
            for h in range(2):
                nc.vector.memset(gram_ps[:, h, :], 0.0).then_inc(gram_free, 1)

            def split(k):
                dve.wait_ge(raw_landed[k % RAWS], 16 * (k // RAWS + 1))
                if k >= 2:
                    dve.wait_ge(hi_ready, k - 1)
                nc.vector.tensor_scalar(top[k % 2].bitcast(I32), raw[k % RAWS].bitcast(I32), -(1 << LOW_BITS), None,
                                        ALU.bitwise_and).then_inc(top_ready, 1)
                dve.wait_ge(top_ready, k + 1)
                nc.vector.tensor_tensor(tab_lo[:VP, k].rearrange("p c d -> p (c d)"), raw[k % RAWS], top[k % 2],
                                        ALU.subtract).then_inc(lo_ready, 1)

            def compare(it, a, k):
                g = ONEHOT * (2 * it + a) + k
                dve.wait_ge(ids_relative, g + 1)
                if not (isinstance(g, int) and g < 2):
                    dve.wait_ge(hot_looked, g - 1)
                for c in range(CH):
                    eq = nc.vector.tensor_scalar(hot[:VP, k % 2, c], ids_near[:VP, a % 2, k], float(c), None,
                                                 ALU.is_equal)
                eq.then_inc(hot_ready, 1)

            def gram_out(it, a, l):
                if l == 0 and not (isinstance(it, int) and (it, a) == (0, 0)):
                    dve.wait_ge(dots_stored, 32 * (2 * it + a))
                for h in range(2):
                    dve.wait_ge(gram_done, 2 * tile_of(it, a, l) + h + 1)
                    i0 = l * NI + h * HI
                    nc.vector.tensor_copy(
                        gram[:, :, i0:i0 + HI],
                        gram_ps[:, h, 0:HI * NV].rearrange("p (i n) -> p n i", n=NV)).then_inc(gram_free, 1)

            def gram_last_out(l):
                for h in range(2):
                    dve.wait_ge(gram_done, 2 * (TILES - 2 + l) + h + 1)
                    dots_v = gram_ps[:, h, 0:HI * NV].rearrange("p (i n) -> p n i", n=NV)
                    nc.vector.tensor_copy(gram_last[l][:, 0:NV, h * HI:(h + 1) * HI], dots_v)
                    nc.vector.tensor_copy(gram_last[l][:, NV:WIDE, h * HI:(h + 1) * HI], dots_v[:, 0:HALF]
                                          ).then_inc(gram_free, 1)

            def unit(it, a, ahead=True):
                for k in range(2, NR + 2):
                    compare(it, a + 1, k)
                gram_out(it, a, 0)
                for k in range(NR + 2, ONEHOT):
                    compare(it, a + 1, k)
                if ahead:
                    compare(it, a + 2, 0)
                gram_out(it, a, 1)
                if ahead:
                    compare(it, a + 2, 1)

            for k in range(RAWS):
                split(k)
            for k in range(ONEHOT):
                if k + RAWS < ONEHOT:
                    split(k + RAWS)
                compare(0, 0, k)
            compare(0, 1, 0)
            compare(0, 1, 1)
            gram_out(0, 0, 0)
            compare(0, 1, 2)
            gram_out(0, 0, 1)
            for k in range(3, ONEHOT):
                compare(0, 1, k)
            compare(0, 2, 0)
            compare(0, 2, 1)
            unit(0, 1)
            with dve.Fori(1, UNITS // 2 - 1) as it:
                unit(it, 0)
                unit(it, 1)
            unit(UNITS // 2 - 1, 0, ahead=False)
            for l in range(2):
                gram_last_out(l)

        @block.scalar
        def _(act):
            nc.scalar.nop().then_inc(look_free, RING)
            ids_t_v = ids_t.rearrange("p u (j l i) -> p u l j i", j=NJ, l=2)
            for u in range(UNITS):
                act.wait_ge(ids_turned, u // 2 + 1)
                nc.scalar.copy(ids_t_v[:, u], ids_bank(u)[0:ONEHOT].rearrange("p (l j i) -> p l j i", l=2, j=NJ)
                               ).then_inc(ids_t_ready, 1)

            def hi_out(k):
                act.wait_ge(top_ready, k + 1)
                nc.scalar.copy(tab_hi[:VP, k].rearrange("p c d -> p (c d)"), top[k % 2]).then_inc(hi_ready, 1)

            def make_relative(it, a, first, end):
                act.wait_ge(ids_near_landed[a % 2], 16 * (it + a // 2 + 1))
                nc.scalar.activation(ids_near[:VP, a % 2, first:end], ids_near[:VP, a % 2, first:end], ACT.Identity,
                                     bias=minus_row[:VP]).then_inc(ids_relative, end - first)

            def hot_out(it, a, k, order, user=0):
                act.wait_ge(hot_looked, ONEHOT * (2 * it + a) + k + 1)
                nc.scalar.copy(T[:, a % 2, :, onehot[k] + 1], look_ps[:, bank_of(user, ("look", k), order), 0:Q]
                               ).then_inc(look_free, 1)

            def turn_out(it, a, l, first_round, end_round, order):
                for r in range(first_round, end_round):
                    n, cnt = rounds[r][0], len(rounds[r])
                    act.wait_ge(turned, 2 * NR + NR * tile_of(it, a, l) + r + 1)
                    nc.scalar.copy(T_tile[a % 2][l][:, n:n + cnt],
                                   look_ps[:, bank_of(a, ("turn", l, r), order), 0:cnt * P].rearrange(
                                       "p (n j i) -> p n j i", n=cnt, j=NJ)).then_inc(look_free, 1)

            def h1_out(it, a, half):
                act.wait_ge(weights_landed, WEIGHTS)
                act.wait_ge(l1_done, 2 * (2 * it + a) + half + 1)
                for f in range(half * F1C // 2, (half + 1) * F1C // 2):
                    nc.scalar.activation(h1[:, f], mlp_ps[:, half, f % 2], ACT.Relu, bias=bias1[:, f:f + 1]
                                         ).then_inc(h1_ready, 1)

            def h2_out(it, a):
                act.wait_ge(l2_done, 2 * it + a + 1)
                for f in range(F2C):
                    nc.scalar.activation(h2[:, f].rearrange("p l (j i) -> p j l i", j=NJ),
                                         mlp_ps[:, 0, f].rearrange("p (j l i) -> p j l i", j=NJ, l=2),
                                         ACT.Relu, bias=bias2[:, f:f + 1]
                                         ).then_inc(h2_ready, 1)

            def y_out(it, a):
                act.wait_ge(l3_done, 2 * it + a + 1)
                nc.scalar.copy(y[:, bass.ds(tile_of(it, a, 0), 2)], mlp_ps[:, 1, 0, 0:2]).then_inc(y_ready, 1)

            def unit(it, a, layer2=True, ahead=True):
                for r in range(NR):
                    turn_out(it, a, 0, r, r + 1, ORDER)
                    if layer2 and r == NR - 2:
                        h2_out(it, a - 2)
                    if layer2 and r == NR - 1:
                        y_out(it, a - 2)
                    hot_out(it, a + 1, r, ORDER, a)
                turn_out(it, a, 1, 0, 1, ORDER)
                hot_out(it, a + 1, NR, ORDER, a)
                if ahead:
                    make_relative(it, a + 2, 0, ONEHOT // 2)
                turn_out(it, a, 1, 1, 3, ORDER)
                if ahead:
                    make_relative(it, a + 2, ONEHOT // 2, ONEHOT)
                h1_out(it, a - 1, 0)
                for k in range(NR + 1, ONEHOT - 1):
                    hot_out(it, a + 1, k, ORDER, a)
                turn_out(it, a, 1, 3, NR, ORDER)
                h1_out(it, a - 1, 1)
                hot_out(it, a + 1, ONEHOT - 1, ORDER, a)

            for k in range(RAWS):
                hi_out(k)
            act.wait_ge(minus_row_ready, 1)
            make_relative(0, 0, 0, 1)
            hi_out(RAWS)
            make_relative(0, 0, 1, ONEHOT)
            for k in range(ONEHOT):
                if k > 0 and k + RAWS < ONEHOT:
                    hi_out(k + RAWS)
                if k == EARLY:
                    turn_out(0, 0, 0, 0, NR, START)
                hot_out(0, 0, k, START)
                if k == EARLY:
                    make_relative(0, 1, 0, ONEHOT)
            turn_out(0, 0, 1, 0, NR, FIRST)
            for k in range(ONEHOT):
                hot_out(0, 1, k, FIRST)
                if k == NR:
                    make_relative(0, 2, 0, ONEHOT)
            unit(0, 1, layer2=False)
            with act.Fori(1, UNITS // 2 - 1) as it:
                unit(it, 0)
                unit(it, 1)
            end = UNITS // 2 - 1
            unit(end, 0, ahead=False)

            def last_h1_out(l):
                for half in range(2):
                    act.wait_ge(l1_done, 2 * (UNITS - 1) + 2 * l + half + 1)
                    for f in range(half * F1C // 2, (half + 1) * F1C // 2):
                        nc.scalar.activation(h1[:, f, l * P:(l + 1) * P], last_l1(l, f), ACT.Relu,
                                             bias=bias1[:, f:f + 1]).then_inc(h1_ready, 1)

            def last_h2_out(l):
                act.wait_ge(l2_done, UNITS + l)
                for f in range(F2C):
                    nc.scalar.activation(h2[:, f, l], last_l2(l, f), ACT.Relu, bias=bias2[:, f:f + 1]
                                         ).then_inc(h2_ready, 1)

            def last_y_out(l):
                act.wait_ge(l3_done, UNITS + l)
                nc.scalar.copy(y[:, TILES - 2 + l:TILES - 1 + l], last_l3(l)).then_inc(y_ready, 1)

            turn_out(end, 1, 0, 0, NR - 1, LAST)
            h2_out(end, -1)
            turn_out(end, 1, 0, NR - 1, NR, LAST)
            y_out(end, -1)
            h1_out(end, 0, 0)
            h1_out(end, 0, 1)
            turn_out(end, 1, 1, 0, NR, LAST)
            h2_out(end, 0)
            last_h1_out(0)
            y_out(end, 0)
            last_h2_out(0)
            last_h1_out(1)
            last_y_out(0)
            last_h2_out(1)
            last_y_out(1)

        @block.tensor
        def _(pe):
            nc.tensor.nop().then_inc(turned, 2 * NR)

            def lookup(it, a, k, order, users):
                pe.wait_ge(hot_ready, ONEHOT * (2 * it + a) + k + 1)
                if order is START:
                    pe.wait_ge(hi_ready, k + 1)
                    pe.wait_ge(lo_ready, k + 1)
                pe.wait_ge(look_free, use_of(*users, ("look", k), order) + 1)
                for c in range(CH):
                    for half, w in enumerate((tab_hi, tab_lo)):
                        mm = pe.matmul(look_ps[:, bank_of(users[1], ("look", k), order), 0:Q], w[:VP, k, c], hot[:VP, k % 2, c],
                                       start=(c == 0 and half == 0), stop=(c == CH - 1 and half == 1))
                mm.then_inc(hot_looked, 1)

            def turn(it, a, l, first_round, end_round, order):
                use = 2 * it + a + 1
                for r in range(first_round, end_round):
                    if 0 in rounds[r]:
                        pe.wait_ge(dense_landed[l], 16 * use)
                    pe.wait_ge(rows_landed[l][r], 16 * (len(rounds[r]) - (0 in rounds[r])) * use)
                    pe.wait_ge(look_free, use_of(it, a, ("turn", l, r), order) + 1)
                    bank = bank_of(a, ("turn", l, r), order)
                    for i, n in enumerate(rounds[r]):
                        mm = pe.transpose(look_ps[:, bank, i * P:(i + 1) * P], rows[:, l, place[n], :], ident[:])
                    mm.then_inc(turned, 1)

            def products(it, a, l, last_use, order):
                t = tile_of(it, a, l)
                pe.wait_ge(look_free, RING + use_of(it, a, last_use, order) + 1)
                for h in range(2):
                    pe.wait_ge(gram_free, 2 * t + h + 1)
                    for i in range(HI):
                        for j in range(NJ):
                            q = (j * 2 + l) * NI + h * HI + i
                            mm = pe.matmul(gram_ps[32 * j:32 * j + NV, h, i * NV:(i + 1) * NV],
                                           T[:, a % 2, q, :], T[:, a % 2, q, 0:NV], start=True, stop=True)
                    mm.then_inc(gram_done, 1)

            def layer1(it, a, first, end):
                for i in range(first, end):
                    f, c = i // (PC + 1), i % (PC + 1)
                    if i == 0:
                        pe.wait_ge(weights_landed, WEIGHTS)
                        pe.wait_ge(shuffled[a % 2], SHUFFLED * (it + a // 2 + 1))
                    kk = P if c == PC else KP
                    rhs = T[:, a % 2, :, 0] if c == PC else pairs[:kk, a % 2, c]
                    mm = pe.matmul(mlp_ps[:, f * 2 // F1C, f % 2], w1[:kk, c, f * P:(f + 1) * P], rhs,
                                   start=(c == 0), stop=(c == PC))
                    if c == PC and f % 2 == 1:
                        mm.then_inc(l1_done, 1)

            def layer2(it, a, first, end):
                for i in range(first, end):
                    f, c = i // F1C, i % F1C
                    if i == 0:
                        pe.wait_ge(h1_ready, F1C * (2 * it + a + 1))
                    mm = pe.matmul(mlp_ps[:, 0, f], w2[:, c, f * P:(f + 1) * P], h1[:, c],
                                   start=(c == 0), stop=(c == F1C - 1))
                    if i == F2C * F1C - 1:
                        mm.then_inc(l2_done, 1)

            def layer3(it, a):
                pe.wait_ge(h2_ready, F2C * (2 * it + a + 1))
                for l in range(2):
                    for c in range(F2C):
                        mm = pe.matmul(mlp_ps[:, 1, 0, l:l + 1], h2[:, c, l], w3[:, c:c + 1],
                                       start=(c == 0), stop=(c == F2C - 1))
                mm.then_inc(l3_done, 1)

            def unit(it, a, mlp2=True):
                for r in range(NR):
                    turn(it, a, 0, r, r + 1, ORDER)
                    if mlp2 and r < NR - 1:
                        layer2(it, a - 2, L2_CUT[r], L2_CUT[r + 1])
                    if mlp2 and r == NR - 1:
                        layer3(it, a - 2)
                    lookup(it, a + 1, r, ORDER, (it, a))
                products(it, a, 0, turns[0][-1], ORDER)
                for r in range(NR):
                    turn(it, a, 1, r, r + 1, ORDER)
                    layer1(it, a - 1, L1_CUT[r], L1_CUT[r + 1])
                    if r == 0:
                        lookup(it, a + 1, NR, ORDER, (it, a))
                    if r == 2:
                        for k in range(NR + 1, ONEHOT - 1):
                            lookup(it, a + 1, k, ORDER, (it, a))
                products(it, a, 1, turns[1][-1], ORDER)
                lookup(it, a + 1, ONEHOT - 1, ORDER, (it, a))

            L2_CUT = [r * F2C * F1C // (NR - 1) for r in range(NR)]
            L1_CUT = [r * F1C * (PC + 1) // NR for r in range(NR + 1)]

            pe.wait_ge(ident_ready, 1)
            pe.wait_ge(ids_hot_ready, 3)
            for t in range(TILES):
                mm = pe.transpose(ids_bank(t // 2)[:, (t % 2) * P:(t % 2 + 1) * P],
                                  ids_hot[:, t * ONEHOT:t * ONEHOT + P], ident[:])
                if t % 4 == 3:
                    mm.then_inc(ids_turned, 1)
            pe.wait_ge(ids_t_ready, UNITS)
            for k in range(ONEHOT):
                if k == EARLY:
                    turn(0, 0, 0, 0, NR, START)
                lookup(0, 0, k, START, (0, 0))
            turn(0, 0, 1, 0, NR, FIRST)
            for k in range(ONEHOT):
                lookup(0, 1, k, FIRST, (0, 0))
                if k == 0:
                    products(0, 0, 0, START[-1], START)
                if k == 1:
                    products(0, 0, 1, turns[1][-1], FIRST)
            unit(0, 1, mlp2=False)
            with pe.Fori(1, UNITS // 2 - 1) as it:
                unit(it, 0)
                unit(it, 1)
            end = UNITS // 2 - 1
            unit(end, 0)

            def last_layer1(l):
                pe.wait_ge(shuffled_last[l], SHUFFLED_LAST)
                dense = T[:, 1].rearrange("p (j l i) n -> p l j i n", j=NJ, l=2)[:, l, :, :, 0]
                for f in range(F1C):
                    for c in range(PC + 1):
                        kk = P if c == PC else KP
                        mm = pe.matmul(last_l1(l, f), w1[:kk, c, f * P:(f + 1) * P],
                                       dense if c == PC else pairs[:kk, 1, c, l * P:(l + 1) * P],
                                       start=(c == 0), stop=(c == PC))
                    if f % 2 == 1:
                        mm.then_inc(l1_done, 1)

            def last_layer2(l):
                for f in range(F2C):
                    for c in range(F1C):
                        if f == 0:
                            pe.wait_ge(h1_ready, F1C * (UNITS - 1 + l) + c + 1)
                        mm = pe.matmul(last_l2(l, f), w2[:, c, f * P:(f + 1) * P], h1[:, c, l * P:(l + 1) * P],
                                       start=(c == 0), stop=(c == F1C - 1))
                mm.then_inc(l2_done, 1)

            def last_layer3(l):
                pe.wait_ge(h2_ready, F2C * (UNITS + l))
                for c in range(F2C):
                    mm = pe.matmul(last_l3(l), h2[:, c, l], w3[:, c:c + 1], start=(c == 0), stop=(c == F2C - 1))
                mm.then_inc(l3_done, 1)

            for r in range(NR - 1):
                turn(end, 1, 0, r, r + 1, LAST)
                layer2(end, -1, L2_CUT[r], L2_CUT[r + 1])
            turn(end, 1, 0, NR - 1, NR, LAST)
            layer3(end, -1)
            products(end, 1, 0, turns[0][-1], LAST)
            layer1(end, 0, 0, F1C * (PC + 1) // 2)
            pe.wait_ge(y_ready, UNITS - 2)
            layer1(end, 0, F1C * (PC + 1) // 2, F1C * (PC + 1))
            turn(end, 1, 1, 0, NR, LAST)
            layer2(end, 0, 0, F1C)
            products(end, 1, 1, turns[1][-1], LAST)
            layer2(end, 0, F1C, F2C * F1C)
            last_layer1(0)
            layer3(end, 0)
            last_layer2(0)
            pe.wait_ge(y_ready, UNITS - 1)
            last_layer1(1)
            last_layer3(0)
            last_layer2(1)
            last_layer3(1)


_INS = ['r_dense', 'ids'] + [f'tbl_{i}' for i in range(26)] + ['W_top1', 'b_top1', 'W_top2', 'b_top2', 'W_top3']


def kernel(**inputs):
    import numpy as _np
    import concourse.bacc as _bacc
    from concourse import mybir as _mybir
    from concourse.bass_utils import run_bass_kernel_spmd as _run

    nc = _bacc.Bacc("TRN2", target_bir_lowering=False, num_devices=1)
    arrays, args = {}, []
    for name in _INS:
        a = _np.ascontiguousarray(inputs[name])
        arrays[f"in_{name}_dram"] = a
        args.append(nc.dram_tensor(f"in_{name}_dram", a.shape, _mybir.dt.from_np(a.dtype), kind="ExternalInput").ap())
    out = nc.dram_tensor("out_0_dram", (inputs['r_dense'].shape[0], 1), _mybir.dt.float32, kind="ExternalOutput").ap()
    dlrm_tower(nc, args[0], args[1], args[2:28], *args[28:33], out)
    r = _run(nc, [arrays], core_ids=[0])
    return r.results[0]["out_0_dram"]
```
